# Optimizing a Trainium2 kernel written in Bass

```python
import numpy as np
import jax
import jax.numpy as jnp

def _softmax(x, axis=-1):
    return jax.nn.softmax(x, axis=axis)

def _gelu(x):
    return jax.nn.gelu(x, approximate=True)

def _silu(x):
    return jax.nn.silu(x)

def _sigmoid(x):
    return jax.nn.sigmoid(x)

def _layernorm(x, axis=-1, eps=1e-05):
    m = jnp.mean(x, axis=axis, keepdims=True)
    v = jnp.var(x, axis=axis, keepdims=True)
    return (x - m) / jnp.sqrt(v + eps)

def _scatter_add(tgt, idx, src, axis=0):
    return tgt.at[idx].add(src)

def _segment_sum(src, seg, n):
    return jax.ops.segment_sum(src, seg, n)
kernel_name = 'mk_prb_d1_jaxref_r8_e9d5bd'

def setup_inputs(seed: int=0):
    np.random.seed(seed)
    _w = jnp.asarray

    def _L0_attn_setup():
        import jax, jax.numpy as jnp
        import numpy as np
        EMB, KDIM, B, S = (128, 64, 8, 256)
        key = jax.random.key(seed)
        kx, kq, kk, kv1, kv2 = jax.random.split(key, 5)

        def xavier(k, shape):
            fan_in, fan_out = shape
            lim = (6.0 / (fan_in + fan_out)) ** 0.5
            return jax.random.uniform(k, shape, jnp.float32, -lim, lim)
        return {'x': jax.random.normal(kx, (B, S, EMB), jnp.float32), 'w_q': xavier(kq, (EMB, KDIM)), 'w_k': xavier(kk, (EMB, KDIM)), 'w_v1': xavier(kv1, (EMB, KDIM)), 'w_v2': xavier(kv2, (KDIM, EMB))}
    _L0_attn_in = _L0_attn_setup()

    def _L0_ffn_setup():
        import jax, jax.numpy as jnp
        import numpy as np
        E = 16
        H = 128
        F = 256
        TOP_K = 1
        B, S = (2, 128)
        key = jax.random.key(seed)
        ks = jax.random.split(key, 7)
        s = 0.02
        return {'hidden_states': jax.random.normal(ks[0], (B, S, H), jnp.float32), 'w_router': jax.random.normal(ks[1], (E, H), jnp.float32) * s, 'gate_up_proj': jax.random.normal(ks[2], (E, H, 2 * F), jnp.float32) * s, 'down_proj': jax.random.normal(ks[3], (E, F, H), jnp.float32) * s, 'w_gate': jax.random.normal(ks[4], (F, H), jnp.float32) * s, 'w_up': jax.random.normal(ks[5], (F, H), jnp.float32) * s, 'w_down': jax.random.normal(ks[6], (H, F), jnp.float32) * s}
    _L0_ffn_in = _L0_ffn_setup()
    _d = {'L0_attn_x': _L0_attn_in['x'], 'L0_attn_w_q': _L0_attn_in['w_q'], 'L0_attn_w_k': _L0_attn_in['w_k'], 'L0_attn_w_v1': _L0_attn_in['w_v1'], 'L0_attn_w_v2': _L0_attn_in['w_v2'], 'L0_ffn_w_router': _L0_ffn_in['w_router'], 'L0_ffn_gate_up_proj': _L0_ffn_in['gate_up_proj'], 'L0_ffn_down_proj': _L0_ffn_in['down_proj'], 'L0_ffn_w_gate': _L0_ffn_in['w_gate'], 'L0_ffn_w_up': _L0_ffn_in['w_up'], 'L0_ffn_w_down': _L0_ffn_in['w_down']}
    _x0 = _d['L0_attn_x']
    _d['L0_attn_x'] = jax.random.normal(jax.random.fold_in(jax.random.key(seed), 1), (4, 1024, 128), dtype=_x0.dtype)
    del _x0
    return _d

def reference(L0_attn_x, L0_attn_w_q, L0_attn_w_k, L0_attn_w_v1, L0_attn_w_v2, L0_ffn_w_router, L0_ffn_gate_up_proj, L0_ffn_down_proj, L0_ffn_w_gate, L0_ffn_w_up, L0_ffn_w_down):

    def _L0_attn_ref(x, w_q, w_k, w_v1, w_v2):
        import jax, jax.numpy as jnp
        import numpy as np
        EMB, KDIM, B, S = (128, 64, 8, 256)
        seq = x.shape[1]
        queries = jnp.einsum('bse,ek->bsk', x, w_q)
        keys = jnp.einsum('bse,ek->bsk', x, w_k)
        scale = w_q.shape[1] ** (-0.5)
        scores = jnp.einsum('bqk,bsk->bqs', queries, keys) * scale
        causal = jnp.tril(jnp.ones((seq, seq), dtype=bool))
        scores = jnp.where(causal[None, :, :], scores, -jnp.inf)
        attn = jax.nn.softmax(scores, axis=-1)
        values = jnp.einsum('bsk,ke->bse', jnp.einsum('bse,ek->bsk', x, w_v1), w_v2)
        return jnp.einsum('bqs,bse->bqe', attn, values)

    def _L0_ffn_ref(hidden_states, w_router, gate_up_proj, down_proj, w_gate, w_up, w_down):
        import jax, jax.numpy as jnp
        import numpy as np
        E = 16
        H = 128
        F = 256
        TOP_K = 1
        B, S = (2, 128)
        b, s, h = hidden_states.shape
        x = hidden_states.reshape(-1, h)
        logits = x @ w_router.T
        _, top_idx = jax.lax.top_k(logits, TOP_K)
        mask = jax.nn.one_hot(top_idx, E, dtype=logits.dtype).sum(axis=1)
        scores = jax.nn.sigmoid(logits) * mask
        masked_inputs = scores.T[:, :, None] * x[None, :, :]
        gate_up = jnp.einsum('eth,ehf->etf', masked_inputs, gate_up_proj)
        gate, up = jnp.split(gate_up, 2, axis=-1)
        expert_out = jnp.einsum('etf,efh->eth', up * jax.nn.silu(gate), down_proj)
        shared = jax.nn.silu(x @ w_gate.T) * (x @ w_up.T) @ w_down.T
        out = shared + expert_out.sum(axis=0)
        return out.reshape(b, s, h)
    x = L0_attn_x
    xn = _layernorm(x, axis=-1)
    x = x + _L0_attn_ref(xn, L0_attn_w_q, L0_attn_w_k, L0_attn_w_v1, L0_attn_w_v2) + _L0_ffn_ref(xn, L0_ffn_w_router, L0_ffn_gate_up_proj, L0_ffn_down_proj, L0_ffn_w_gate, L0_ffn_w_up, L0_ffn_w_down)
    return x

_drawn_inputs = setup_inputs


def setup_inputs(seed=0):
    import zlib

    import numpy as np

    out = dict(_drawn_inputs(seed))
    spreads = {}
    factors = {'L0_ffn_w_router': 8.0,
     'L0_ffn_gate_up_proj': 8.0,
     'L0_ffn_down_proj': 8.0,
     'L0_ffn_w_gate': 6.961,
     'L0_ffn_w_up': 6.905,
     'L0_ffn_w_down': 6.879}
    for name, (base, spread) in spreads.items():
        noise = np.random.default_rng([zlib.crc32(name.encode()), seed]).standard_normal(out[name].shape)
        drawn = base * np.exp(spread * noise) if base else spread * noise
        out[name] = jnp.asarray(drawn.astype(out[name].dtype))
    for name, factor in factors.items():
        out[name] = (out[name] * factor).astype(out[name].dtype)
    return out
```

```python
from contextlib import ExitStack

import numpy as np

import concourse.bass as bass
import concourse.mybir as mybir
from concourse.alu_op_type import AluOpType as ALU

ACT = mybir.ActivationFunctionType
AX = mybir.AxisListType
F32 = mybir.dt.float32
F32R = mybir.dt.float32r
BF16 = mybir.dt.bfloat16
I32 = mybir.dt.int32
U32 = mybir.dt.uint32

P = 128
GT = 4
GC = GT * P
EPS = 1e-5
MASKED = -3.0e38
NO_TOKEN = 1 << 20


def build(nc, x, w_small, w_experts, scratch, out):
    B, S, EMB = x.shape
    NT = B * S // P
    NG = NT // GT
    BT = S // P
    BG = BT // GT
    NE, FE = w_experts.shape[1], w_experts.shape[2] // 3
    KD = 64
    FC = FE // P
    NS = scratch.shape[0] // P
    NP = NS // 2
    ROW = P + 1
    VR = KD + NE
    assert EMB == P and BG == 2 and FC == 2
    QK0, VR0, GATE0 = 0, 2 * KD, 2 * KD + VR
    UP0 = GATE0 + FE
    DOWN0 = UP0 + FE
    V20 = DOWN0 + FC * P
    WS = V20 + P
    assert w_small.shape[1] == WS
    WE = 3 * FE
    STEPS = GT + 2 * GT

    with ExitStack() as ctx:
        top = [nc.sbuf_base]

        def at(name, shape, dt, offset):
            return nc.alloc_sbuf_tensor_at(name, shape, dt, offset=offset)

        def size(shape, dt):
            n = 2 if dt == BF16 else 4
            for d in shape[1:]:
                n *= d
            return (n + 31) // 32 * 32

        def sb(name, shape, dt=F32):
            t = at(name, shape, dt, top[0])
            top[0] += size(shape, dt)
            return t

        def overlay(start, parts):
            got = []
            for name, shape, dt in parts:
                got.append(at(name, shape, dt, start))
                start += size(shape, dt)
            return got, start

        top[0] = (top[0] + 31) // 32 * 32
        res = sb("res", [P, NT, P])
        qk_all = sb("qk_all", [P, NT * P])
        vr_all = sb("vr_all", [P, NT, VR])
        wsh = sb("wsh", [P, WS], F32R)
        wsl = sb("wsl", [P, WS], F32R)
        identf = sb("identf", [P, P])
        identb = sb("identb", [P, P], BF16)
        causal = sb("causal", [P, P], BF16)
        before = sb("before", [P, P], BF16)
        onesb = sb("onesb", [P, P], BF16)
        lastf = sb("lastf", [P, NE])
        upto = sb("upto", [P, NE, NE])
        slotno = sb("slotno", [P, NS])
        stats = sb("stats", [P, NT, 6])
        lns = sb("lns", [P, 8, NT])
        minus_half = sb("minus_half", [P, NT])
        score = sb("score", [P, NT])
        slot = sb("slot", [P, NT], U32)
        tile_expert = sb("tile_expert", [1, NS], I32)
        ids = sb("ids", [P, NS], U32)
        blank = sb("blank", [P, ROW])
        w_at = top[0]
        weh, wel = sb("weh", [P, NE, WE], F32R), sb("wel", [P, NE, WE], F32R)
        we_raw = at("we_raw", [P, NE, WE], F32, w_at + size([P, NE, WE], F32))
        (rows, rt_eq, rt_sel, onehot, rt_small, rt_int, ws_raw), end = overlay(w_at, [
            ("rows", [P, NT, ROW], F32), ("rt_eq", [P, NS, NE], F32), ("rt_sel", [P, NT, NE], F32),
            ("onehot", [P, NT, NE], BF16), ("rt_small", [P, 8, NS], F32), ("rt_int", [P, NE], I32),
            ("ws_raw", [P, WS], F32)])
        assert end <= w_at + size([P, NE, WE], F32)
        q_raw = sb("q_raw", [P, S])
        q_hl = sb("q_hl", [P, S], F32R)
        k_hi = sb("k_hi", [P, S], F32R)
        k_lo = sb("k_lo", [P, S], F32R)
        v_raw = sb("v_raw", [P, BT, KD])
        v_hl = sb("v_hl", [P, BT, 2 * KD], F32R)
        negmax, den, rden = sb("negmax", [P, BT]), sb("den", [P, BT]), sb("rden", [P, BT])
        work = top[0]
        a_names = [(f"xn{u}", [P, GT, P], F32) for u in range(2)]
        a_names += [(f"xth{u}", [P, GC], F32R) for u in range(2)]
        a_names += [(f"xtl{u}", [P, GC], F32R) for u in range(2)]
        a_names += [(f"sg{c}", [P, GC], F32) for c in range(FC)]
        a_names += [(f"h{c}", [P, GC], F32) for c in range(FC)]
        a_names += [(f"hh{c}", [P, GC], F32R) for c in range(FC)]
        a_names += [(f"hl{c}", [P, GC], F32R) for c in range(FC)]
        a, a_end = overlay(work, a_names)
        xn, xth, xtl, sg, h, hh, hl = [a[2 * n:2 * n + 2] for n in range(7)]
        c, c_end = overlay(work, [(f"prob{r}", [P, S], F32) for r in range(GT)]
                           + [(f"pth{n}", [P, GC], F32R) for n in range(2)]
                           + [(f"ptl{n}", [P, GC], F32R) for n in range(2)]
                           + [("oth", [P, GC], F32R), ("otl", [P, GC], F32R)])
        prob, pth, ptl, oth, otl = c[:GT], c[4:6], c[6:8], c[8], c[9]
        d, d_end = overlay(work, [(f"xe{q}", [P, 2, ROW], F32) for q in range(2)]
                           + [(f"xeh{q}", [P, 2, P], F32R) for q in range(2)]
                           + [(f"xel{q}", [P, 2, P], F32R) for q in range(2)]
                           + [(f"esg{q}", [P, 2, FE], F32) for q in range(2)]
                           + [(f"eh{q}", [P, 2, FE], F32) for q in range(2)]
                           + [(f"ehh{q}", [P, 2, FC, P], F32R) for q in range(2)]
                           + [(f"ehl{q}", [P, 2, FC, P], F32R) for q in range(2)]
                           + [(f"y{q}", [P, 2, P], F32) for q in range(2)])
        xe, xeh, xel, esg, eh, ehh, ehl, y = [d[2 * n:2 * n + 2] for n in range(8)]
        assert max(a_end, c_end, d_end) <= nc.sbuf_usable_end, (a_end, c_end, d_end)

        def psum(name, cols):
            return ctx.enter_context(nc.psum_tensor(name, [P, cols], F32))

        big = [psum(f"big{n}", 2 * GC) for n in range(2)]
        mid = [psum(f"mid{n}", GC) for n in range(2)]
        acc = [psum(f"acc{n}", GC) for n in range(2)]

        def sem(name, n=None):
            if n is None:
                return ctx.enter_context(nc.semaphore(name))
            return [ctx.enter_context(nc.semaphore(f"{name}{i}")) for i in range(n)]

        NX = 4
        x_loaded = sem("x_loaded", NX)
        ws_loaded, we_loaded = sem("ws_loaded"), sem("we_loaded")
        blanked, scratch_blank = sem("blanked"), sem("scratch_blank")
        const_made, const_step = sem("const_made"), sem("const_step")
        ws_split, ws_hi = sem("ws_split"), sem("ws_hi")
        ln_step, var_ready, rstd_ready = sem("ln_step"), sem("var_ready"), sem("rstd_ready")
        xn_ready, xn_kept, xt_done = sem("xn_ready", 2), sem("xn_kept", 2), sem("xt_done", 2)
        xth_ready, xtl_ready = sem("xth_ready", 2), sem("xtl_ready", 2)
        vr_done, vr_kept = sem("vr_done", 2), sem("vr_kept", 2)
        qk_done, qk_kept = sem("qk_done", 2), sem("qk_kept", 2)
        gu_done, sg_ready, h_ready = sem("gu_done", 2), sem("sg_ready", 2), sem("h_ready", 2)
        hh_ready, hl_ready = sem("hh_ready", 2), sem("hl_ready", 2)
        ffn_done, shared_added = sem("ffn_done"), sem("shared_added", 2)
        rt_step, onehot_ready, ranked = sem("rt_step"), sem("onehot_ready"), sem("ranked")
        top_ready, tanh_ready, score_ready = sem("top_ready"), sem("tanh_ready"), sem("score_ready")
        slots_ready, experts_ready = sem("slots_ready"), sem("experts_ready")
        row_scaled, row_sent = sem("row_scaled"), sem("row_sent")
        weh_ready, wel_ready = sem("weh_ready"), sem("wel_ready")
        raw_ready, q_hi_ready, q_lo_ready = sem("raw_ready"), sem("q_hi_ready"), sem("q_lo_ready")
        k_hi_ready, k_lo_ready = sem("k_hi_ready"), sem("k_lo_ready")
        v_hi_ready, v_lo_ready = sem("v_hi_ready"), sem("v_lo_ready")
        s_done, max_ready, exp_done = sem("s_done"), sem("max_ready"), sem("exp_done")
        pt_done, pth_ready, ptl_ready = sem("pt_done"), sem("pth_ready"), sem("ptl_ready")
        pv_done, rden_ready = sem("pv_done"), sem("rden_ready")
        oth_ready, otl_ready = sem("oth_ready"), sem("otl_ready")
        proj_done, att_added, out_written = sem("proj_done"), sem("att_added", 2), sem("out_written")
        xe_loaded, ids_kept = sem("xe_loaded", 2), sem("ids_kept")
        xet_done, xeh_ready, xel_ready = sem("xet_done"), sem("xeh_ready"), sem("xel_ready")
        egu_done, esg_ready, eh_ready = sem("egu_done"), sem("esg_ready"), sem("eh_ready")
        eht_done, ehh_ready, ehl_ready = sem("eht_done"), sem("ehh_ready"), sem("ehl_ready")
        ey_done, y_ready, y_added = sem("ey_done"), sem("y_ready"), sem("y_added", 2)

        primed = [ffn_done, *xt_done, *xn_kept, *hl_ready, *h_ready, *shared_added, *vr_kept, *qk_kept, s_done,
                  q_lo_ready, v_lo_ready, pv_done, pt_done, rden_ready, proj_done, exp_done, ptl_ready, *att_added]
        out_rows = out.rearrange("b s e -> (b s) e")
        out_tiles = out_rows.rearrange("(t p) e -> p t e", p=P)
        x_tiles = x.rearrange("b (t p) e -> p (b t) e", p=P)
        block = ctx.enter_context(nc.Block())

        def flat(ap):
            return ap.rearrange("p a b -> p (a b)")

        def staged(eng, step):
            for p in range(4):
                step(p, p % 2)
            with eng.Fori(2, NP // 2 - 1) as i:
                for q in range(2):
                    step(2 * i + q, q, True)
            for p in range(NP - 2, NP + 2):
                step(p, p % 2)

        def live(p, loop, lo, hi):
            return loop or lo <= p < hi

        @block.sync
        def _(sp):
            n = NT // NX
            for k in range(NX):
                sp.dma_start(res[:, k * n:(k + 1) * n, :], x_tiles[:, k * n:(k + 1) * n, :]
                             ).then_inc(x_loaded[k], 16)
                if k == 0:
                    sp.dma_start(ws_raw[:, :], w_small).then_inc(ws_loaded, 16)
            sp.wait_ge(blanked, 2)
            sp.dma_start(scratch.rearrange("(t p) r -> p t r", p=P),
                         blank[:, None, :].to_broadcast([P, NS, ROW])).then_inc(scratch_blank, 16)
            sp.dma_start(we_raw[:, :, :], w_experts).then_inc(we_loaded, 16)
            for u in range(2):
                sp.wait_ge(qk_kept[u], FIRST + NG // 2)
                sp.wait_ge(vr_kept[u], FIRST + NG // 2)
            with sp.Fori(0, B) as b:
                col, tile0 = sp.snap(b * S), sp.snap(b * BT)
                out_tile = [sp.snap(b * BT + g * GT) for g in range(BG)]
                round_ = sp.snap(b + 1)
                sp.wait_ge(s_done, FIRST + tile0)
                for half in range(2):
                    at_half = slice(half * KD, (half + 1) * KD)
                    sp.dma_start(q_raw[at_half, :], qk_all[0:KD, bass.ds(col, S)]).then_inc(raw_ready, 16)
                    sp.dma_start(k_lo[at_half, :].bitcast(F32),
                                 qk_all[KD:P, bass.ds(col, S)]).then_inc(raw_ready, 16)
                sp.wait_ge(v_lo_ready, FIRST + b)
                sp.dma_start(v_raw[:, :, :], vr_all[:, bass.ds(tile0, BT), 0:KD]).then_inc(raw_ready, 16)
                for g in range(BG):
                    sp.wait_ge(att_added[g], FIRST + 1 + b)
                    t = out_tile[g]
                    sp.dma_start(out_tiles[:, bass.ds(t, GT), :], res[:, bass.ds(t, GT), :]
                                 ).then_inc(out_written, 16)

            sp.wait_ge(row_sent, 16 * NT)
            sp.wait_ge(ptl_ready, FIRST + B * STEPS)
            sp.wait_ge(oth_ready, B * BG)
            sp.wait_ge(proj_done, FIRST + B * BG)

            def load(first_slot, q):
                sp.dma_start(xe[q][:, :, :],
                             scratch[bass.ds(first_slot, 2 * P), :].rearrange("(v p) r -> p v r", p=P)
                             ).then_inc(xe_loaded[q], 16)

            for q in range(2):
                load(q * 2 * P, q)
            with sp.Fori(1, NP // 2) as i:
                first_slot = [sp.snap((2 * i + q) * 2 * P) for q in range(2)]
                used = [sp.snap(2 * i + q - 1) for q in range(2)]
                for q in range(2):
                    sp.wait_ge(xet_done, used[q])
                    sp.wait_ge(ids_kept, used[q])
                    load(first_slot[q], q)
            sp.wait_ge(out_written, 16 * B * BG)
            sp.wait_ge(scratch_blank, 16)
            for q in range(2):
                sp.wait_ge(y_added[q], 16 * NP)

        @block.gpsimd
        def _(pool):
            for s in primed:
                pool.sem_inc(s, FIRST)
            pool.memset(blank[:, 0:P], 0.0).then_inc(blanked, 1)
            pool.memset(blank[:, P:ROW].bitcast(I32), NO_TOKEN).then_inc(blanked, 1)
            pool.memset(identf[:, :], 0.0).then_inc(const_step, 1)
            pool.memset(identb[:, :], 0.0).then_inc(const_step, 1)
            pool.memset(causal[:, :], 0.0).then_inc(const_step, 1)
            pool.memset(before[:, :], 1.0).then_inc(const_step, 1)
            pool.memset(upto[:, :, :], 1.0).then_inc(const_step, 1)
            pool.memset(onesb[:, :], 1.0).then_inc(const_made, 1)
            pool.memset(minus_half[:, :], -0.5).then_inc(const_made, 1)
            pool.wait_ge(const_step, 5)
            for m in (identf, identb):
                pool.affine_select(out=m[:, :], in_=m[:, :], compare_op=ALU.not_equal, fill=1.0, base=0,
                                   pattern=[[-1, P]], channel_multiplier=1).then_inc(const_made, 1)
            pool.affine_select(out=causal[:, :], in_=causal[:, :], compare_op=ALU.is_ge, fill=MASKED, base=0,
                               pattern=[[-1, P]], channel_multiplier=1).then_inc(const_made, 1)
            pool.affine_select(out=before[:, :], in_=before[:, :], compare_op=ALU.is_gt, fill=0.0, base=0,
                               pattern=[[1, P]], channel_multiplier=-1).then_inc(const_made, 1)
            pool.affine_select(out=upto[:, :, :], in_=upto[:, :, :], compare_op=ALU.is_ge, fill=0.0, base=0,
                               pattern=[[1, NE], [-1, NE]], channel_multiplier=0).then_inc(const_made, 1)
            pool.iota(lastf[:, :], pattern=[[-1, NE]], base=NE, channel_multiplier=0,
                      allow_small_or_imprecise_dtypes=True).then_inc(const_made, 1)
            pool.iota(slotno[:, :], pattern=[[1, NS]], base=0, channel_multiplier=0,
                      allow_small_or_imprecise_dtypes=True).then_inc(const_made, 1)
            pool.iota(rows[:, :, P].bitcast(I32), pattern=[[P, NT]], base=0, channel_multiplier=1
                      ).then_inc(const_made, 1)
            pool.wait_ge(var_ready, 1)
            pool.wait_ge(const_made, CONSTS)
            pool.tensor_tensor(lns[:, 7, :], lns[:, 6, :], minus_half[:, :], ALU.pow).then_inc(rstd_ready, 1)
            with pool.Fori(0, NG // 2) as b:
                for u in range(2):
                    pool.wait_ge(xn_ready[u], b + 1)
                    pool.tensor_copy(rows[:, bass.ds((2 * b + u) * GT, GT), 0:P], xn[u][:, :, :]
                                     ).then_inc(xn_kept[u], 1)
                for u in range(2):
                    g = 2 * b + u
                    for c in range(FC):
                        pool.wait_ge(hh_ready[c], g + 1)
                        pool.wait_ge(ffn_done, FIRST + g)
                        pool.tensor_tensor(hl[c][:, :], h[c][:, :], hh[c][:, :].bitcast(F32), ALU.subtract
                                           ).then_inc(hl_ready[c], 1)
            pool.wait_ge(score_ready, 1)
            pool.wait_ge(slots_ready, 1)
            pool.wait_ge(scratch_blank, 16)
            for u in range(2):
                pool.wait_ge(xn_kept[u], FIRST + NG // 2)
            for t in range(NT):
                pool.tensor_scalar(rows[:, t, 0:P], rows[:, t, 0:P], score[:, t:t + 1], None, ALU.mult
                                   ).then_inc(row_scaled, 1)
                pool.wait_ge(row_scaled, t + 1)
                pool.indirect_dma_start(scratch, bass.IndirectOffsetOnAxis(ap=slot[:, t:t + 1], axis=0),
                                        rows[:, t, :], None).then_inc(row_sent, 16)
            with pool.Fori(0, B) as b:
                pool.wait_ge(v_hi_ready, b + 1)
                pool.tensor_tensor(v_hl[:, :, KD:2 * KD], v_raw[:, :, :], v_hl[:, :, 0:KD].bitcast(F32),
                                   ALU.subtract).then_inc(v_lo_ready, 1)
            pool.wait_ge(we_loaded, 16)
            pool.wait_ge(row_sent, 16 * NT)
            pool.wait_ge(experts_ready, 1)
            with pool.Fori(0, NE) as e:
                pool.tensor_copy(flat(weh[:, bass.ds(e, 1), :]), flat(we_raw[:, bass.ds(e, 1), :])
                                 ).then_inc(weh_ready, 1)
            pool.wait_ge(weh_ready, NE)
            with pool.Fori(0, NE) as e:
                pool.tensor_tensor(flat(wel[:, bass.ds(e, 1), :]), flat(we_raw[:, bass.ds(e, 1), :]),
                                   flat(weh[:, bass.ds(e, 1), :]).bitcast(F32), ALU.subtract
                                   ).then_inc(wel_ready, 1)
            pool.wait_ge(out_written, 16 * B * BG)
            for p in range(NP + 1):
                if p < NP:
                    pool.wait_ge(xe_loaded[p % 2], 16 * (p // 2 + 1))
                    pool.tensor_copy(ids[:, 2 * p:2 * p + 2], xe[p % 2][:, :, P].bitcast(U32)
                                     ).then_inc(ids_kept, 1)
                if p:
                    pool.wait_ge(ids_kept, p)
                    pool.wait_ge(y_ready, p)
                    for v in range(2):
                        t = 2 * (p - 1) + v
                        pool.indirect_dma_start(out_rows, bass.IndirectOffsetOnAxis(ap=ids[:, t:t + 1], axis=0),
                                                y[(p - 1) % 2][:, v, :], None, bounds_check=NT * P - 1,
                                                oob_is_err=False, compute_op=ALU.add).then_inc(y_added[(p - 1) % 2], 16)

        @block.vector
        def _(dve):
            n = NT // NX
            for k in range(NX):
                dve.wait_ge(x_loaded[k], 16)
                for t in range(k * n, (k + 1) * n):
                    dve.bn_stats(stats[:, t, :], res[:, t, :]).then_inc(ln_step, 1)
                if k == 0:
                    dve.wait_ge(ws_loaded, 16)
                    dve.tensor_copy(wsh[:, :], ws_raw[:, :]).then_inc(ws_hi, 1)
                    dve.wait_ge(ws_hi, 1)
                    dve.tensor_tensor(wsl[:, :], ws_raw[:, :], wsh[:, :].bitcast(F32), ALU.subtract
                                      ).then_inc(ws_split, 1)
            dve.wait_ge(ln_step, NT)
            mean_e, m2_e, mean_o, m2_o = (stats[:, :, i] for i in (1, 2, 4, 5))
            total, mean, diff, sq, m2, both, var, rstd = (lns[:, i, :] for i in range(8))
            dve.tensor_tensor(total, mean_e, mean_o, ALU.add).then_inc(ln_step, 1)
            dve.tensor_tensor(diff, mean_e, mean_o, ALU.subtract).then_inc(ln_step, 1)
            dve.tensor_tensor(m2, m2_e, m2_o, ALU.add).then_inc(ln_step, 1)
            dve.wait_ge(ln_step, NT + 3)
            dve.tensor_scalar(mean, total, 0.5, None, ALU.mult).then_inc(ln_step, 1)
            dve.tensor_tensor(sq, diff, diff, ALU.mult).then_inc(ln_step, 1)
            dve.wait_ge(ln_step, NT + 5)
            dve.scalar_tensor_tensor(out=both, in0=sq, scalar=P / 4, in1=m2, op0=ALU.mult, op1=ALU.add
                                     ).then_inc(ln_step, 1)
            dve.wait_ge(ln_step, NT + 6)
            dve.tensor_scalar(var, both, 1.0 / P, EPS, ALU.mult, ALU.add).then_inc(var_ready, 1)
            dve.wait_ge(rstd_ready, 1)
            with dve.Fori(0, NG // 2) as b:
                for u in range(2):
                    t0 = (2 * b + u) * GT
                    dve.wait_ge(xt_done[u], FIRST + b)
                    dve.wait_ge(xn_kept[u], FIRST + b)
                    for t in range(GT):
                        last = dve.tensor_scalar(xn[u][:, t, :], flat(res[:, bass.ds(t0 + t, 1), :]),
                                                 mean[:, bass.ds(t0 + t, 1)], rstd[:, bass.ds(t0 + t, 1)],
                                                 ALU.subtract, ALU.mult)
                    last.then_inc(xn_ready[u], 1)
                for u in range(2):
                    dve.wait_ge(xth_ready[u], b + 1)
                    dve.tensor_tensor(xtl[u][:, :], acc[u][:, :], xth[u][:, :].bitcast(F32), ALU.subtract
                                      ).then_inc(xtl_ready[u], 1)
                for u in range(2):
                    g = 2 * b + u
                    for c in range(FC):
                        dve.wait_ge(sg_ready[c], g + 1)
                        dve.wait_ge(hl_ready[c], FIRST + g)
                        dve.tensor_tensor(h[c][:, :], sg[c][:, :], big[c][:, GC:2 * GC], ALU.mult
                                          ).then_inc(h_ready[c], 1)
                    dve.wait_ge(ffn_done, FIRST + g + 1)
                    r = flat(res[:, bass.ds(g * GT, GT), :])
                    dve.tensor_tensor(r, acc[u][:, :], r, ALU.add).then_inc(shared_added[u], 1)
            for u in range(2):
                dve.wait_ge(vr_kept[u], FIRST + NG // 2)
            dve.wait_ge(const_made, CONSTS)
            logits = vr_all[:, :, KD:VR]
            step = [0]

            def done(ins):
                step[0] += 1
                ins.then_inc(rt_step, 1)
                dve.wait_ge(rt_step, step[0])

            highest, first, slotf = (rt_small[:, i, 0:NT] for i in range(3))
            counts, tiles, upto_tiles, start = (rt_small[:, i, 0:NE] for i in range(3, 7))
            over = rt_small[0:1, 7, 0:NS]
            te = rt_eq[:, 0:NT, :]

            def spread(ap, n):
                return ap[:, :, None].to_broadcast([ap.shape[0], ap.shape[1], n])

            def repeat(ap, n):
                return ap[:, None, :].to_broadcast([ap.shape[0], n, ap.shape[1]])

            dve.tensor_reduce(highest, logits, AX.X, ALU.max).then_inc(top_ready, 1)
            dve.wait_ge(top_ready, 1)
            done(dve.tensor_tensor(te, logits, spread(highest, NE), ALU.is_equal))
            done(dve.tensor_tensor(rt_sel[:, :, :], te, repeat(lastf[:, :], NT), ALU.mult))
            done(dve.tensor_reduce(first, rt_sel[:, :, :], AX.X, ALU.max))
            dve.tensor_tensor(onehot[:, :, :], rt_sel[:, :, :], spread(first, NE), ALU.is_equal
                              ).then_inc(onehot_ready, 1)
            dve.wait_ge(tanh_ready, 1)
            dve.tensor_scalar(score[:, :], score[:, :], 0.5, 0.5, ALU.mult, ALU.add).then_inc(score_ready, 1)
            dve.wait_ge(ranked, 1)
            done(dve.tensor_reduce(counts, big[1][:, 0:NT * NE].rearrange("p (t e) -> p e t", e=NE), AX.X, ALU.add))
            done(dve.tensor_scalar(rt_int[:, :], counts, float(P - 1), None, ALU.add))
            done(dve.tensor_scalar(rt_int[:, :], rt_int[:, :], 7, None, ALU.logical_shift_right))
            done(dve.tensor_copy(tiles, rt_int[:, :]))
            done(dve.tensor_tensor(rt_sel[:, 0:NE, :], upto[:, :, :], repeat(tiles, NE), ALU.mult))
            done(dve.tensor_reduce(upto_tiles, rt_sel[:, 0:NE, :], AX.X, ALU.add))
            done(dve.tensor_tensor(start, upto_tiles, tiles, ALU.subtract))
            done(dve.tensor_scalar(start, start, float(P), None, ALU.mult))
            done(dve.tensor_tensor(rt_sel[:, :, :], big[0][:, 0:NT * NE].rearrange("p (t e) -> p t e", e=NE),
                                   repeat(start, NT), ALU.add))
            done(dve.tensor_tensor(rt_sel[:, :, :], rt_sel[:, :, :], onehot[:, :, :], ALU.mult))
            done(dve.tensor_reduce(slotf, rt_sel[:, :, :], AX.X, ALU.add))
            dve.tensor_copy(slot[:, :], slotf).then_inc(slots_ready, 1)
            done(dve.tensor_tensor(rt_eq[0:1, :, :], spread(slotno[0:1, :], NE), repeat(upto_tiles[0:1, :], NS),
                                   ALU.is_ge))
            done(dve.tensor_reduce(over, rt_eq[0:1, :, :], AX.X, ALU.add))
            dve.tensor_scalar(tile_expert[:, :], over, float(NE - 1), None, ALU.min).then_inc(experts_ready, 1)
            for u in range(2):
                dve.wait_ge(shared_added[u], FIRST + NG // 2)
            with dve.Fori(0, B) as b:
                dve.wait_ge(q_hi_ready, b + 1)
                dve.scalar_tensor_tensor(out=q_hl[KD:P, :], in0=q_raw[KD:P, :], scalar=float(KD) ** -0.5,
                                         in1=q_hl[KD:P, :].bitcast(F32), op0=ALU.mult, op1=ALU.subtract
                                         ).then_inc(q_lo_ready, 1)
                dve.wait_ge(k_hi_ready, b + 1)
                dve.tensor_tensor(k_lo[:, :], k_lo[:, :].bitcast(F32), k_hi[:, :].bitcast(F32), ALU.subtract
                                  ).then_inc(k_lo_ready, 1)

                def row_max(i):
                    dve.wait_ge(s_done, FIRST + b * BT + i + 1)
                    dve.tensor_reduce(negmax[:, i:i + 1], big[i % 2][:, 0:(i + 1) * P], AX.X, ALU.max,
                                      negate=True).then_inc(max_ready, 1)

                def probs_lo(n):
                    _, c0 = block_of(n)
                    dve.wait_ge(pth_ready, b * STEPS + n + 1)
                    dve.wait_ge(pv_done, FIRST + b * STEPS + max(n - 1, 0))
                    dve.tensor_tensor(ptl[n % 2][:, c0:GC], mid[n % 2][:, c0:GC],
                                      pth[n % 2][:, c0:GC].bitcast(F32), ALU.subtract).then_inc(ptl_ready, 1)

                def out_lo(g):
                    dve.wait_ge(oth_ready, b * BG + g + 1)
                    dve.tensor_tensor(otl[:, :], acc[g][:, :], oth[:, :].bitcast(F32), ALU.subtract
                                      ).then_inc(otl_ready, 1)

                def add(g):
                    dve.reciprocal(rden[:, g * GT:(g + 1) * GT], den[:, g * GT:(g + 1) * GT]
                                   ).then_inc(rden_ready, 1)
                    dve.wait_ge(rden_ready, FIRST + b * BG + g + 1)
                    dve.wait_ge(proj_done, FIRST + b * BG + g + 1)
                    for t in range(GT):
                        r = flat(res[:, bass.ds(b * BT + g * GT + t, 1), :])
                        last = dve.scalar_tensor_tensor(
                            out=r, in0=acc[g][:, t * P:(t + 1) * P], scalar=rden[:, g * GT + t:g * GT + t + 1],
                            in1=r, op0=ALU.mult, op1=ALU.add)
                    last.then_inc(att_added[g], 1)

                for i in range(GT):
                    row_max(i)
                for n in range(GT):
                    probs_lo(n)
                    row_max(GT + n)
                out_lo(0)
                probs_lo(GT)
                add(0)
                for n in range(GT + 1, STEPS):
                    probs_lo(n)
                out_lo(1)
                add(1)

            def step(p, q, loop=False):
                if live(p - 1, loop, 0, NP):
                    dve.wait_ge(ehh_ready, p)
                    dve.tensor_tensor(ehl[1 - q][:, :, :, :].rearrange("p v c t -> p (v c t)"), mid[1][:, :],
                                      ehh[1 - q][:, :, :, :].rearrange("p v c t -> p (v c t)").bitcast(F32),
                                      ALU.subtract).then_inc(ehl_ready, 1)
                if live(p, loop, 0, NP):
                    dve.wait_ge(esg_ready, p + 1)
                    dve.tensor_tensor(eh[q][:, :, :], esg[q][:, :, :],
                                      big[q][:, :].rearrange("p (v f) -> p v f", v=2)[:, :, FE:2 * FE],
                                      ALU.mult).then_inc(eh_ready, 1)
                if live(p + 1, loop, 0, NP):
                    dve.wait_ge(xeh_ready, p + 2)
                    dve.tensor_tensor(flat(xel[1 - q][:, :, :]), mid[0][:, 0:2 * P],
                                      flat(xeh[1 - q][:, :, :]).bitcast(F32), ALU.subtract
                                      ).then_inc(xel_ready, 1)

            dve.wait_ge(xeh_ready, 1)
            dve.tensor_tensor(flat(xel[0][:, :, :]), mid[0][:, 0:2 * P], flat(xeh[0][:, :, :]).bitcast(F32),
                              ALU.subtract).then_inc(xel_ready, 1)
            staged(dve, step)

        @block.scalar
        def _(act):
            with act.Fori(0, NG // 2) as b:
                for u in range(2):
                    act.wait_ge(xt_done[u], FIRST + b + 1)
                    act.wait_ge(ffn_done, FIRST + 2 * b)
                    act.copy(xth[u][:, :], acc[u][:, :]).then_inc(xth_ready[u], 1)
                for u in range(2):
                    g = 2 * b + u
                    act.wait_ge(vr_done[u], b + 1)
                    act.copy(vr_all[:, bass.ds(g * GT, GT), :],
                             mid[0][:, 0:GT * VR].rearrange("p (t n) -> p t n", t=GT)).then_inc(vr_kept[u], 1)
                    act.wait_ge(qk_done[u], b + 1)
                    act.copy(qk_all[:, bass.ds(g * GC, GC)], mid[1][:, :]).then_inc(qk_kept[u], 1)
                    for c in range(FC):
                        act.wait_ge(gu_done[c], g + 1)
                        act.wait_ge(h_ready[c], FIRST + g)
                        act.activation(sg[c][:, :], big[c][:, 0:GC], ACT.Silu).then_inc(sg_ready[c], 1)
                    for c in range(FC):
                        act.wait_ge(h_ready[c], FIRST + g + 1)
                        act.wait_ge(ffn_done, FIRST + g)
                        act.copy(hh[c][:, :], h[c][:, :]).then_inc(hh_ready[c], 1)
            act.wait_ge(top_ready, 1)
            act.activation(score[:, :], rt_small[:, 0, 0:NT], ACT.Tanh, scale=0.5).then_inc(tanh_ready, 1)
            for u in range(2):
                act.wait_ge(shared_added[u], FIRST + NG // 2)
            with act.Fori(0, B) as b:
                act.wait_ge(raw_ready, 80 * b + 80)
                act.wait_ge(s_done, FIRST + b * BT)
                act.mul(q_hl[:, :], q_raw[:, :], float(KD) ** -0.5).then_inc(q_hi_ready, 1)
                act.copy(k_hi[:, :], k_lo[:, :].bitcast(F32)).then_inc(k_hi_ready, 1)
                act.wait_ge(pv_done, FIRST + b * STEPS)
                act.copy(v_hl[:, :, 0:KD], v_raw[:, :, :]).then_inc(v_hi_ready, 1)

                def exp(i):
                    act.wait_ge(max_ready, b * BT + i + 1)
                    act.wait_ge(pt_done, FIRST + b * STEPS + max(i - GT + 1, 0))
                    act.wait_ge(rden_ready, FIRST + b * BG)
                    act.activation(prob[i % GT][:, 0:(i + 1) * P], big[i % 2][:, 0:(i + 1) * P], ACT.Exp,
                                   bias=negmax[:, i:i + 1], accum_out=den[:, i:i + 1]).then_inc(exp_done, 1)

                def probs_hi(n):
                    _, c0 = block_of(n)
                    act.wait_ge(pt_done, FIRST + b * STEPS + n + 1)
                    act.wait_ge(pv_done, FIRST + b * STEPS + max(n - 1, 0))
                    act.copy(pth[n % 2][:, c0:GC], mid[n % 2][:, c0:GC]).then_inc(pth_ready, 1)

                def out_hi(g):
                    act.wait_ge(pv_done, FIRST + b * STEPS + (STEPS if g else GT))
                    act.wait_ge(proj_done, FIRST + b * BG + g)
                    act.copy(oth[:, :], acc[g][:, :]).then_inc(oth_ready, 1)

                for i in range(GT):
                    exp(i)
                for n in range(GT):
                    probs_hi(n)
                    exp(GT + n)
                out_hi(0)
                for n in range(GT, STEPS):
                    probs_hi(n)
                out_hi(1)

            def step(p, q, loop=False):
                if live(p - 1, loop, 0, NP):
                    act.wait_ge(eht_done, p)
                    act.wait_ge(ey_done, max(p - 2, 0) if not loop else p - 2)
                    act.copy(ehh[1 - q][:, :, :, :].rearrange("p v c t -> p (v c t)"), mid[1][:, :]
                             ).then_inc(ehh_ready, 1)
                if live(p - 2, loop, 0, NP):
                    act.wait_ge(ey_done, p - 1)
                    act.wait_ge(y_added[q], 16 * (p - 2 - q))
                    act.copy(flat(y[q][:, :, :]), acc[q][:, 0:2 * P]).then_inc(y_ready, 1)
                if live(p, loop, 0, NP):
                    act.wait_ge(egu_done, 2 * p + 2)
                    act.activation(esg[q][:, :, :], big[q][:, :].rearrange("p (v f) -> p v f", v=2)[:, :, 0:FE],
                                   ACT.Silu).then_inc(esg_ready, 1)
                if live(p + 1, loop, 0, NP):
                    act.wait_ge(xet_done, p + 2)
                    act.wait_ge(egu_done, 2 * p)
                    act.copy(flat(xeh[1 - q][:, :, :]), mid[0][:, 0:2 * P]).then_inc(xeh_ready, 1)

            act.wait_ge(xet_done, 1)
            act.copy(flat(xeh[0][:, :, :]), mid[0][:, 0:2 * P]).then_inc(xeh_ready, 1)
            staged(act, step)

        @block.tensor
        def _(pe):
            def product(dst, weights, moving, first=True, final=True):
                (wh, wl), (mh, ml) = weights, moving
                pe.matmul(dst, wh, mh, start=first, stop=False)
                pe.matmul(dst, wh, ml, start=False, stop=False)
                return pe.matmul(dst, wl, mh, start=False, stop=final)

            def small(a0, a1):
                return wsh[:, a0:a1], wsl[:, a0:a1]

            pe.wait_ge(ws_split, 1)
            pe.wait_ge(const_made, CONSTS)
            with pe.Fori(0, NG // 2) as b:
                for u in range(2):
                    pe.wait_ge(xn_ready[u], b + 1)
                    pe.wait_ge(shared_added[u], FIRST + b)
                    for t in range(GT):
                        last = pe.transpose(acc[u][:, t * P:(t + 1) * P], xn[u][:, t, :], identf[:, :])
                    last.then_inc(xt_done[u], 1)

                def down(u):
                    g = 2 * b + u
                    for c in range(FC):
                        pe.wait_ge(hh_ready[c], g + 1)
                        pe.wait_ge(hl_ready[c], FIRST + g + 1)
                    for t in range(GT):
                        for c in range(FC):
                            cols = slice(t * P, (t + 1) * P)
                            last = product(acc[u][:, cols], (hh[c][:, cols], hl[c][:, cols]),
                                           small(DOWN0 + c * P, DOWN0 + (c + 1) * P), c == 0, c == FC - 1)
                    last.then_inc(ffn_done, 1)

                for u in range(2):
                    g = 2 * b + u
                    xt = xth[u], xtl[u]
                    pe.wait_ge(xth_ready[u], b + 1)
                    pe.wait_ge(xtl_ready[u], b + 1)
                    pe.wait_ge(vr_kept[1 - u], FIRST + b + u)
                    for t in range(GT):
                        cols = slice(t * P, (t + 1) * P)
                        last = product(mid[0][:, t * VR:(t + 1) * VR], (xt[0][:, cols], xt[1][:, cols]),
                                       small(VR0, VR0 + VR))
                    last.then_inc(vr_done[u], 1)
                    pe.wait_ge(qk_kept[1 - u], FIRST + b + u)
                    product(mid[1][:, :], small(QK0, QK0 + P), (xt[0][:, :], xt[1][:, :])).then_inc(qk_done[u], 1)
                    if u:
                        down(0)
                    for c in range(FC):
                        pe.wait_ge(h_ready[c], FIRST + g)
                        for n, w0 in enumerate((GATE0, UP0)):
                            last = product(big[c][:, n * GC:(n + 1) * GC], small(w0 + c * P, w0 + (c + 1) * P),
                                           (xt[0][:, :], xt[1][:, :]))
                        last.then_inc(gu_done[c], 1)
                down(1)
            pe.wait_ge(onehot_ready, 1)
            oh = flat(onehot[:, :, :])
            pe.matmul(big[1][:, 0:NT * NE], onesb[:, :], oh, start=True, stop=True)
            pe.matmul(big[0][:, 0:NT * NE], before[:, :], oh, start=True, stop=True, skip_group_check=True)
            for t in range(1, NT):
                last = pe.matmul(big[0][:, t * NE:NT * NE], onesb[:, :], oh[:, 0:(NT - t) * NE], start=False,
                                 stop=True, skip_group_check=True)
            last.then_inc(ranked, 1)
            pe.wait_ge(slots_ready, 1)
            with pe.Fori(0, B) as b:
                def scores(i):
                    if i == 0:
                        pe.wait_ge(q_lo_ready, FIRST + b + 1)
                        pe.wait_ge(k_lo_ready, b + 1)
                    pe.wait_ge(exp_done, FIRST + b * BT + max(i - 1, 0))
                    q = q_hl[:, i * P:(i + 1) * P]
                    for k0 in range(0, (i + 1) * P, GC):
                        k1 = min(k0 + GC, (i + 1) * P)
                        dst = big[i % 2][:, k0:k1]
                        pe.matmul(dst, q, k_hi[:, k0:k1], start=True, stop=False)
                        if k1 == (i + 1) * P:
                            pe.matmul(big[i % 2][:, i * P:k1], identb[:, :], causal[:, :],
                                      start=False, stop=False)
                        last = pe.matmul(dst, q, k_lo[:, k0:k1], start=False, stop=True)
                    last.then_inc(s_done, 1)

                def transposes(n):
                    kb, c0 = block_of(n)
                    g = 0 if n < GT else 1
                    pe.wait_ge(exp_done, FIRST + b * BT + (g + 1) * GT)
                    pe.wait_ge(ptl_ready, FIRST + b * STEPS + max(n - 1, 0))
                    for r in range(c0 // P, GT):
                        last = pe.transpose(mid[n % 2][:, r * P:(r + 1) * P], prob[r][:, kb * P:(kb + 1) * P],
                                            identf[:, :])
                    last.then_inc(pt_done, 1)

                def weigh(n):
                    kb, c0 = block_of(n)
                    g = 0 if n < GT else 1
                    if n == 0:
                        pe.wait_ge(v_lo_ready, FIRST + b + 1)
                    if kb == 0:
                        pe.wait_ge(att_added[g], FIRST + b)
                    pe.wait_ge(ptl_ready, FIRST + b * STEPS + n + 1)
                    pe.matmul(acc[g][:, c0:GC], v_hl[:, kb, :], pth[n % 2][:, c0:GC], start=kb == 0, stop=False,
                              skip_group_check=True)
                    pe.matmul(acc[g][:, c0:GC], v_hl[:, kb, :], ptl[n % 2][:, c0:GC], start=False, stop=True,
                              skip_group_check=True).then_inc(pv_done, 1)

                def project(g):
                    pe.wait_ge(otl_ready, b * BG + g + 1)
                    for t in range(GT):
                        cols = slice(t * P, (t + 1) * P)
                        last = product(acc[g][:, cols], (oth[:, cols], otl[:, cols]), small(V20, V20 + P))
                    last.then_inc(proj_done, 1)

                for i in range(GT):
                    scores(i)
                transposes(0)
                for n in range(GT):
                    scores(GT + n)
                    if n + 1 < GT:
                        transposes(n + 1)
                    weigh(n)
                for n in range(GT, STEPS):
                    if n == GT:
                        transposes(n)
                    if n + 1 < STEPS:
                        transposes(n + 1)
                    if n == GT:
                        project(0)
                    weigh(n)
                project(1)

            def expert(p, v):
                return pe.value_load(tile_expert[0:1, bass.ds(2 * p + v, 1)], min_val=0, max_val=NE - 1)

            def transpose_rows(p, q):
                pe.wait_ge(xe_loaded[q], 8 * (p - q) + 16)
                pe.wait_ge(xel_ready, p)
                for v in range(2):
                    last = pe.transpose(mid[0][:, v * P:(v + 1) * P], xe[q][:, v, 0:P], identf[:, :])
                last.then_inc(xet_done, 1)

            def gate_up(p, q, v):
                e = expert(p, v)
                if v == 0:
                    pe.wait_ge(xel_ready, p + 1)
                w = [flat(m[:, bass.ds(e, 1), 0:2 * FE]) for m in (weh, wel)]
                product(big[q][:, v * GC:(v + 1) * GC], (xeh[q][:, v, :], xel[q][:, v, :]), w
                        ).then_inc(egu_done, 1)

            def transpose_hidden(p, q):
                pe.wait_ge(eh_ready, p + 1)
                pe.wait_ge(ehl_ready, p)
                for v in range(2):
                    for c in range(FC):
                        n = v * FC + c
                        last = pe.transpose(mid[1][:, n * P:(n + 1) * P], eh[q][:, v, c * P:(c + 1) * P],
                                            identf[:, :])
                last.then_inc(eht_done, 1)

            def down(p, q):
                pe.wait_ge(ehl_ready, p + 1)
                pe.wait_ge(y_ready, p)
                for v in range(2):
                    e = expert(p, v)
                    for c in range(FC):
                        cols = slice(2 * FE + c * P, 2 * FE + (c + 1) * P)
                        w = [flat(m[:, bass.ds(e, 1), cols]) for m in (weh, wel)]
                        last = product(acc[q][:, v * P:(v + 1) * P], (ehh[q][:, v, c, :], ehl[q][:, v, c, :]), w,
                                       c == 0, c == FC - 1)
                last.then_inc(ey_done, 1)

            def step(p, q, loop=False):
                if live(p, loop, 0, NP):
                    gate_up(p, q, 0)
                if live(p - 1, loop, 0, NP):
                    transpose_hidden(p - 1, 1 - q)
                if live(p - 2, loop, 0, NP):
                    down(p - 2, q)
                if live(p, loop, 0, NP):
                    gate_up(p, q, 1)
                if live(p + 1, loop, 0, NP):
                    transpose_rows(p + 1, 1 - q)

            pe.wait_ge(wel_ready, NE)
            pe.wait_ge(experts_ready, 1)
            transpose_rows(0, 0)
            staged(pe, step)


CONSTS = 10
FIRST = 1


def block_of(n):
    kb = n if n < GT else n - GT
    return kb, (kb if n < GT else max(kb - GT, 0)) * P


def kernel(L0_attn_x, L0_attn_w_q, L0_attn_w_k, L0_attn_w_v1, L0_attn_w_v2, L0_ffn_w_router,
           L0_ffn_gate_up_proj, L0_ffn_down_proj, L0_ffn_w_gate, L0_ffn_w_up, L0_ffn_w_down):
    import concourse.bacc as bacc
    from concourse.bass_utils import run_bass_kernel_spmd

    x = np.ascontiguousarray(L0_attn_x)
    F = L0_ffn_w_down.shape[1]
    E = L0_ffn_down_proj.shape[0]
    w_down = np.transpose(L0_ffn_w_down).reshape(F // P, P, P).transpose(1, 0, 2).reshape(P, F)
    w_small = np.ascontiguousarray(np.concatenate([
        L0_attn_w_q, L0_attn_w_k, L0_attn_w_v1, np.transpose(L0_ffn_w_router), np.transpose(L0_ffn_w_gate),
        np.transpose(L0_ffn_w_up), w_down, np.concatenate([L0_attn_w_v2, L0_attn_w_v2], axis=0)], axis=1))
    gate_up = np.transpose(L0_ffn_gate_up_proj, (1, 0, 2))
    down = np.reshape(L0_ffn_down_proj, (E, F // P, P, P)).transpose(2, 0, 1, 3).reshape(P, E, F)
    w_experts = np.ascontiguousarray(np.concatenate([gate_up, down], axis=2))

    n_tokens = x.shape[0] * x.shape[1]
    slot_tiles = n_tokens // P + E
    nc = bacc.Bacc("TRN2", target_bir_lowering=False, num_devices=1)
    arrays = {"x": x, "w_small": w_small, "w_experts": w_experts}
    args = [nc.dram_tensor(n, a.shape, F32, kind="ExternalInput").ap() for n, a in arrays.items()]
    scratch = nc.dram_tensor("scratch", (slot_tiles * P, P + 1), F32, kind="Internal").ap()
    out = nc.dram_tensor("out", x.shape, F32, kind="ExternalOutput").ap()
    build(nc, *args, scratch, out)
    return run_bass_kernel_spmd(nc, [arrays], core_ids=[0]).results[0]["out"]
```

```python
from contextlib import ExitStack

import numpy as np

import concourse.bass as bass
import concourse.mybir as mybir
from concourse.alu_op_type import AluOpType as ALU

ACT = mybir.ActivationFunctionType
AX = mybir.AxisListType
F32 = mybir.dt.float32
F32R = mybir.dt.float32r
BF16 = mybir.dt.bfloat16
I32 = mybir.dt.int32
U32 = mybir.dt.uint32

P = 128
GT = 4
GC = GT * P
EPS = 1e-5
MASKED = -3.0e38
NO_TOKEN = 1 << 20


def build(nc, x, w_small, w_gate_up, w_down, scratch, out):
    B, S, EMB = x.shape
    NT = B * S // P
    NG = NT // GT
    BT = S // P
    BG = BT // GT
    NE, FE = w_down.shape[1], w_down.shape[2]
    KD = 64
    FC = FE // P
    NS = scratch.shape[0] // P
    NP = NS // 2
    ROW = P + 1
    VR = KD + NE
    EB = NE // B
    assert NE == 1 << CODE and EMB == P and BG == 2 and FC == 2 and w_gate_up.shape[2] == GC
    QK0, VR0, GATE0 = 0, 2 * KD, 2 * KD + VR
    UP0 = GATE0 + FE
    DOWN0 = UP0 + FE
    V20 = DOWN0 + FC * P
    WS = V20 + P
    assert w_small.shape[1] == WS
    STEPS = GT + 2 * GT

    with ExitStack() as ctx:
        top = [(nc.sbuf_base + 31) // 32 * 32]

        def size(shape, dt):
            n = 2 if dt == BF16 else 4
            for d in shape[1:]:
                n *= d
            return (n + 31) // 32 * 32

        def sb(name, shape, dt=F32):
            t = nc.alloc_sbuf_tensor_at(name, shape, dt, offset=top[0])
            top[0] += size(shape, dt)
            return t

        def overlay(start, parts):
            got = []
            for name, shape, dt in parts:
                got.append(nc.alloc_sbuf_tensor_at(name, shape, dt, offset=start))
                start += size(shape, dt)
            return got, start

        res = sb("res", [P, NT, P])
        rows = sb("rows", [P, NT, ROW])
        qk_all = sb("qk_all", [P, NT * P])
        vr_all = sb("vr_all", [P, NT, VR])
        ws_raw = sb("ws_raw", [P, WS])
        wsh = sb("wsh", [P, DOWN0], F32R)
        wsl = sb("wsl", [P, DOWN0], F32R)
        weh = sb("weh", [P, NE, 2 * FE], F32R)
        we_raw = nc.alloc_sbuf_tensor_at("we_raw", [P, NE, 2 * FE], F32, offset=top[0])
        wel = sb("wel", [P, NE, 2 * FE], F32R)
        wed = sb("wed", [P, NE, FE])
        identf = sb("identf", [P, P])
        identb = sb("identb", [P, P], BF16)
        causal = sb("causal", [P, P], BF16)
        before = sb("before", [P, P], BF16)
        onesb = sb("onesb", [P, P], BF16)
        lastf = sb("lastf", [P, NE])
        upto = sb("upto", [P, NE, NE])
        slotno = sb("slotno", [P, NS])
        stats = sb("stats", [P, NT, 6])
        ln = [sb(f"ln{i}", [P, NT]) for i in range(8)]
        minus_half = sb("minus_half", [P, BT])
        highest, score = sb("highest", [P, NT]), sb("score", [P, NT])
        onehot = sb("onehot", [P, NT, NE], BF16)
        slot = sb("slot", [P, NT], U32)
        pair_code = sb("pair_code", [1, 2 + NP + 2])
        step_experts = sb("step_experts", [1, NP + 2], I32)
        ids = sb("ids", [P, NS], U32)
        blank = sb("blank", [P, ROW])
        xe = [sb(f"xe{q}", [P, 2, ROW]) for q in range(2)]
        q_raw = sb("q_raw", [P, S])
        q_hl = sb("q_hl", [P, S], F32R)
        k_hi = sb("k_hi", [P, S], F32R)
        k_lo = sb("k_lo", [P, S], F32R)
        v_raw = sb("v_raw", [P, BT, KD])
        v_hl = sb("v_hl", [P, BT, 2 * KD], F32R)
        negmax, den, rden = sb("negmax", [P, BT]), sb("den", [P, BT]), sb("rden", [P, BT])
        a, a_end = overlay(top[0], [(f"xn{u}", [P, GT, P], F32) for u in range(2)]
                           + [(f"xth{u}", [P, GC], F32R) for u in range(2)]
                           + [(f"xtl{u}", [P, GC], F32R) for u in range(2)]
                           + [(f"sg{c}", [P, GC], F32) for c in range(FC)]
                           + [(f"h{c}", [P, GC], F32) for c in range(FC)])
        xn, xth, xtl, sg, h = [a[2 * n:2 * n + 2] for n in range(5)]
        (rt_eq, rt_sel, rt_small, rt_int), b_end = overlay(a_end, [
            ("rt_eq", [P, NS, NE], F32), ("rt_sel", [P, NT, NE], F32), ("rt_small", [P, 8, NS], F32),
            ("rt_int", [P, NE], I32)])
        c, c_end = overlay(top[0], [(f"prob{r}", [P, S], F32) for r in range(GT)]
                           + [(f"pth{n}", [P, GC], F32R) for n in range(2)]
                           + [(f"ptl{n}", [P, GC], F32R) for n in range(2)] + [("ot", [P, GC], F32)])
        prob, pth, ptl, ot = c[:GT], c[4:6], c[6:8], c[8]
        d, d_end = overlay(top[0], [(f"xeh{q}", [P, 2, P], F32R) for q in range(2)]
                           + [(f"xel{q}", [P, 2, P], F32R) for q in range(2)]
                           + [(f"esg{q}", [P, 2, FE], F32) for q in range(2)]
                           + [(f"eh{q}", [P, 2, FE], F32) for q in range(2)]
                           + [(f"eht{q}", [P, 2, FC, P], F32) for q in range(2)]
                           + [(f"y{q}", [P, 2, P], F32) for q in range(2)])
        xeh, xel, esg, eh, eht, y = [d[2 * n:2 * n + 2] for n in range(6)]
        assert max(b_end, c_end, d_end) <= nc.sbuf_usable_end, (b_end, c_end, d_end, nc.sbuf_usable_end)

        def psum(name, cols):
            return ctx.enter_context(nc.psum_tensor(name, [P, cols], F32))

        big = [psum(f"big{n}", 2 * GC) for n in range(2)]
        mid = [psum(f"mid{n}", GC) for n in range(2)]
        acc = [psum(f"acc{n}", GC) for n in range(2)]

        def sem(name, n=None):
            if n is None:
                return ctx.enter_context(nc.semaphore(name))
            return [ctx.enter_context(nc.semaphore(f"{name}{i}")) for i in range(n)]

        x_loaded, we_loaded, wed_loaded = sem("x_loaded", B), sem("we_loaded", B), sem("wed_loaded")
        ws_loaded = sem("ws_loaded")
        blanked, scratch_blank = sem("blanked"), sem("scratch_blank")
        const_made, const_step = sem("const_made"), sem("const_step")
        ws_split, ws_hi = sem("ws_split"), sem("ws_hi")
        ln_step, var_ready, rstd_ready = sem("ln_step"), sem("var_ready"), sem("rstd_ready")
        xn_ready, rows_kept, xt_done = sem("xn_ready", 2), sem("rows_kept", 2), sem("xt_done", 2)
        xth_ready, xtl_ready = sem("xth_ready", 2), sem("xtl_ready", 2)
        vr_done, vr_kept = sem("vr_done", 2), sem("vr_kept", 2)
        qk_done, qk_kept = sem("qk_done", 2), sem("qk_kept", 2)
        gu_done, sg_ready, h_ready = sem("gu_done", 2), sem("sg_ready", 2), sem("h_ready", 2)
        ffn_done, shared_added = sem("ffn_done"), sem("shared_added", 2)
        top_ready, tanh_ready, score_ready = sem("top_ready"), sem("tanh_ready"), sem("score_ready")
        hot_step, onehot_ready = sem("hot_step"), sem("onehot_ready")
        weh_ready, wel_ready = sem("weh_ready"), sem("wel_ready")
        rt_step, ranked = sem("rt_step"), sem("ranked")
        slots_ready, experts_ready = sem("slots_ready"), sem("experts_ready")
        row_sent = sem("row_sent")
        raw_ready, q_hi_ready, q_lo_ready = sem("raw_ready"), sem("q_hi_ready"), sem("q_lo_ready")
        k_hi_ready, k_lo_ready = sem("k_hi_ready"), sem("k_lo_ready")
        v_hi_ready, v_lo_ready = sem("v_hi_ready"), sem("v_lo_ready")
        s_done, max_ready, exp_done = sem("s_done"), sem("max_ready"), sem("exp_done")
        pt_done, pth_ready, ptl_ready = sem("pt_done"), sem("pth_ready"), sem("ptl_ready")
        pv_done, rden_ready, ot_ready = sem("pv_done"), sem("rden_ready", 2), sem("ot_ready")
        proj_done, att_added, out_written = sem("proj_done"), sem("att_added", 2), sem("out_written")
        xe_loaded, ids_kept = sem("xe_loaded", 2), sem("ids_kept")
        xet_done, xeh_ready, xel_ready = sem("xet_done"), sem("xeh_ready"), sem("xel_ready")
        egu_done, esg_ready, eh_ready = sem("egu_done"), sem("esg_ready"), sem("eh_ready")
        eht_done, eht_ready = sem("eht_done"), sem("eht_ready")
        ey_done, y_ready, y_added = sem("ey_done"), sem("y_ready"), sem("y_added", 2)

        primed = [ffn_done, *xt_done, *rows_kept, *h_ready, *shared_added, *vr_kept, *qk_kept, s_done,
                  q_lo_ready, v_lo_ready, pv_done, pt_done, *rden_ready, proj_done, exp_done, ptl_ready, *att_added]
        out_rows = out.rearrange("b s e -> (b s) e")
        out_tiles = out_rows.rearrange("(t p) e -> p t e", p=P)
        x_tiles = x.rearrange("b (t p) e -> p (b t) e", p=P)
        block = ctx.enter_context(nc.Block())

        def flat(ap):
            return ap.rearrange("p a b -> p (a b)")

        def spread(ap, n):
            return ap[:, :, None].to_broadcast([ap.shape[0], ap.shape[1], n])

        def repeat(ap, n):
            return ap[:, None, :].to_broadcast([ap.shape[0], n, ap.shape[1]])

        def phase_a(eng, step, between=None):
            step(0, True)
            with eng.Fori(1, B - 1) as b:
                step(b, True)
            if between:
                between()
            step(B - 1, False)

        def phase_c(eng, first_half, second_half, routing=None):
            first_half(0, True)
            if routing:
                routing()
            with eng.Fori(1, B) as b:
                second_half(b - 1, b)
                first_half(b, False)
            second_half(B - 1, None)

        def phase_d(eng, step):
            for p in range(4):
                step(p, p % 2)
            with eng.Fori(2, NP // 2 - 1) as i:
                for q in range(2):
                    step(2 * i + q, q, True)
            for p in range(NP - 2, NP + 2):
                step(p, p % 2)

        def live(p, loop):
            return loop or 0 <= p < NP

        @block.sync
        def _(sp):
            def load_x(b):
                sp.dma_start(res[:, b * BT:(b + 1) * BT, :], x_tiles[:, b * BT:(b + 1) * BT, :]
                             ).then_inc(x_loaded[b], 16)

            load_x(0)
            sp.dma_start(ws_raw[:, :], w_small).then_inc(ws_loaded, 16)
            load_x(1)
            for b in range(B):
                if b >= 2:
                    load_x(b)
                e = slice(b * EB, (b + 1) * EB)
                sp.dma_start(we_raw[:, e, :], w_gate_up[:, e, :]).then_inc(we_loaded[b], 16)
            sp.wait_ge(blanked, 2)
            sp.dma_start(scratch.rearrange("(t p) r -> p t r", p=P),
                         blank[:, None, :].to_broadcast([P, NS, ROW])).then_inc(scratch_blank, 16)
            sp.dma_start(wed[:, :, :], w_down).then_inc(wed_loaded, 16)

            def load_raw(b, col, tile0):
                for half in range(2):
                    at_half = slice(half * KD, (half + 1) * KD)
                    sp.dma_start(q_raw[at_half, :], qk_all[0:KD, bass.ds(col, S)]).then_inc(raw_ready, 16)
                    sp.dma_start(k_lo[at_half, :].bitcast(F32), qk_all[KD:P, bass.ds(col, S)]
                                 ).then_inc(raw_ready, 16)
                if isinstance(b, int) and b == 0:
                    for u in range(2):
                        sp.wait_ge(vr_kept[u], FIRST + 1)
                else:
                    sp.wait_ge(v_lo_ready, FIRST + b)
                sp.dma_start(v_raw[:, :, :], vr_all[:, bass.ds(tile0, BT), 0:KD]).then_inc(raw_ready, 16)

            def store(t):
                sp.dma_start(out_tiles[:, bass.ds(t, GT), :], res[:, bass.ds(t, GT), :]).then_inc(out_written, 16)

            for u in range(2):
                sp.wait_ge(qk_kept[u], FIRST + 1)
            load_raw(0, 0, 0)
            for u in range(2):
                sp.wait_ge(qk_kept[u], FIRST + B)
                sp.wait_ge(vr_kept[u], FIRST + B)
            with sp.Fori(1, B) as b:
                col, tile0 = sp.snap(b * S), sp.snap(b * BT)
                out_tile = [sp.snap((b - 1) * BT + g * GT) for g in range(BG)]
                sp.wait_ge(s_done, FIRST + tile0)
                load_raw(b, col, tile0)
                for g in range(BG):
                    sp.wait_ge(att_added[g], FIRST + b)
                    store(out_tile[g])
            for g in range(BG):
                sp.wait_ge(att_added[g], FIRST + B)
                store((B - 1) * BT + g * GT)

            sp.wait_ge(row_sent, 16 * NT)

            def load_rows(first_slot, q):
                sp.dma_start(xe[q][:, :, :],
                             scratch[bass.ds(first_slot, 2 * P), :].rearrange("(v p) r -> p v r", p=P)
                             ).then_inc(xe_loaded[q], 16)

            for q in range(2):
                load_rows(q * 2 * P, q)
            with sp.Fori(1, NP // 2) as i:
                first_slot = [sp.snap((2 * i + q) * 2 * P) for q in range(2)]
                used = [sp.snap(2 * i + q - 1) for q in range(2)]
                for q in range(2):
                    sp.wait_ge(xet_done, used[q])
                    sp.wait_ge(ids_kept, used[q])
                    load_rows(first_slot[q], q)
            sp.wait_ge(out_written, 16 * B * BG)
            sp.wait_ge(scratch_blank, 16)
            for q in range(2):
                sp.wait_ge(y_added[q], 16 * NP)

        @block.gpsimd
        def _(pool):
            for s in primed:
                pool.sem_inc(s, FIRST)
            pool.memset(identf[:, :], 0.0).then_inc(const_step, 1)
            pool.memset(minus_half[:, :], -0.5).then_inc(const_made, 1)
            pool.wait_ge(const_step, 1)
            pool.affine_select(out=identf[:, :], in_=identf[:, :], compare_op=ALU.not_equal, fill=1.0, base=0,
                               pattern=[[-1, P]], channel_multiplier=1).then_inc(const_made, 1)

            def rsqrt(b):
                pool.wait_ge(var_ready, b + 1)
                t = bass.ds(b * BT, BT)
                pool.tensor_tensor(ln[7][:, t], ln[6][:, t], minus_half[:, :], ALU.pow).then_inc(rstd_ready, 1)

            pool.wait_ge(const_made, 2)
            rsqrt(0)
            pool.memset(blank[:, 0:P], 0.0).then_inc(blanked, 1)
            pool.memset(pair_code[:, :], 0.0).then_inc(const_made, 1)
            pool.memset(blank[:, P:ROW].bitcast(I32), NO_TOKEN).then_inc(blanked, 1)
            pool.memset(identb[:, :], 0.0).then_inc(const_step, 1)
            pool.memset(causal[:, :], 0.0).then_inc(const_step, 1)
            pool.memset(before[:, :], 1.0).then_inc(const_step, 1)
            pool.memset(upto[:, :, :], 1.0).then_inc(const_step, 1)
            pool.memset(onesb[:, :], 1.0).then_inc(const_made, 1)
            pool.wait_ge(const_step, 5)
            pool.affine_select(out=identb[:, :], in_=identb[:, :], compare_op=ALU.not_equal, fill=1.0, base=0,
                               pattern=[[-1, P]], channel_multiplier=1).then_inc(const_made, 1)
            pool.affine_select(out=causal[:, :], in_=causal[:, :], compare_op=ALU.is_ge, fill=MASKED, base=0,
                               pattern=[[-1, P]], channel_multiplier=1).then_inc(const_made, 1)
            pool.affine_select(out=before[:, :], in_=before[:, :], compare_op=ALU.is_gt, fill=0.0, base=0,
                               pattern=[[1, P]], channel_multiplier=-1).then_inc(const_made, 1)
            pool.affine_select(out=upto[:, :, :], in_=upto[:, :, :], compare_op=ALU.is_ge, fill=0.0, base=0,
                               pattern=[[1, NE], [-1, NE]], channel_multiplier=0).then_inc(const_made, 1)
            pool.iota(lastf[:, :], pattern=[[-1, NE]], base=NE, channel_multiplier=0,
                      allow_small_or_imprecise_dtypes=True).then_inc(const_made, 1)
            pool.iota(slotno[:, :], pattern=[[1, NS]], base=0, channel_multiplier=0,
                      allow_small_or_imprecise_dtypes=True).then_inc(const_made, 1)
            pool.iota(rows[:, :, P].bitcast(I32), pattern=[[P, NT]], base=0, channel_multiplier=1
                      ).then_inc(const_made, 1)

            def step(b, more):
                if more:
                    rsqrt(b + 1)
                for u in range(2):
                    t0 = (2 * b + u) * GT
                    pool.wait_ge(score_ready, 2 * b + u + 1)
                    pool.tensor_tensor(rows[:, bass.ds(t0, GT), 0:P], xn[u][:, :, :],
                                       spread(score[:, bass.ds(t0, GT)], P), ALU.mult
                                       ).then_inc(rows_kept[u], 1)

            phase_a(pool, step)
            pool.wait_ge(slots_ready, 1)
            pool.wait_ge(scratch_blank, 16)
            for u in range(2):
                pool.wait_ge(rows_kept[u], FIRST + B)
            for t in range(NT):
                pool.indirect_dma_start(scratch, bass.IndirectOffsetOnAxis(ap=slot[:, t:t + 1], axis=0),
                                        rows[:, t, :], None).then_inc(row_sent, 16)
            pool.wait_ge(out_written, 16 * B * BG)
            for p in range(-AHEAD, NP):
                if p + AHEAD < NP:
                    load = p + AHEAD
                    pool.wait_ge(xe_loaded[load % 2], 16 * (load // 2 + 1))
                    pool.tensor_copy(ids[:, 2 * load:2 * load + 2], xe[load % 2][:, :, P].bitcast(U32)
                                     ).then_inc(ids_kept, 1)
                if p >= 0:
                    pool.wait_ge(ids_kept, p + 1)
                    pool.wait_ge(y_ready, p + 1)
                    for v in range(2):
                        t = 2 * p + v
                        pool.indirect_dma_start(out_rows, bass.IndirectOffsetOnAxis(ap=ids[:, t:t + 1], axis=0),
                                                y[p % 2][:, v, :], None, bounds_check=NT * P - 1,
                                                oob_is_err=False, compute_op=ALU.add
                                                ).then_inc(y_added[p % 2], 16)

        @block.vector
        def _(dve):
            mean_e, m2_e, mean_o, m2_o = (stats[:, :, i] for i in (1, 2, 4, 5))
            total, mean, diff, sq, m2, both, var, rstd = ln
            LN_STEPS = BT + 6

            def statistics(b):
                for t in range(BT):
                    dve.bn_stats(flat(stats[:, bass.ds(b * BT + t, 1), :]), flat(res[:, bass.ds(b * BT + t, 1), :])
                                 ).then_inc(ln_step, 1)
                t = bass.ds(b * BT, BT)
                n0 = b * LN_STEPS
                dve.wait_ge(ln_step, n0 + BT)
                dve.tensor_tensor(total[:, t], mean_e[:, t], mean_o[:, t], ALU.add).then_inc(ln_step, 1)
                dve.tensor_tensor(diff[:, t], mean_e[:, t], mean_o[:, t], ALU.subtract).then_inc(ln_step, 1)
                dve.tensor_tensor(m2[:, t], m2_e[:, t], m2_o[:, t], ALU.add).then_inc(ln_step, 1)
                dve.wait_ge(ln_step, n0 + BT + 3)
                dve.tensor_scalar(mean[:, t], total[:, t], 0.5, None, ALU.mult).then_inc(ln_step, 1)
                dve.tensor_tensor(sq[:, t], diff[:, t], diff[:, t], ALU.mult).then_inc(ln_step, 1)
                dve.wait_ge(ln_step, n0 + BT + 5)
                dve.scalar_tensor_tensor(out=both[:, t], in0=sq[:, t], scalar=P / 4, in1=m2[:, t], op0=ALU.mult,
                                         op1=ALU.add).then_inc(ln_step, 1)
                dve.wait_ge(ln_step, n0 + BT + 6)
                dve.tensor_scalar(var[:, t], both[:, t], 1.0 / P, EPS, ALU.mult, ALU.add).then_inc(var_ready, 1)

            def normalize(b, u):
                t0 = (2 * b + u) * GT
                dve.wait_ge(xt_done[u], FIRST + b)
                dve.wait_ge(rows_kept[u], FIRST + b)
                dve.wait_ge(rstd_ready, b + 1)
                for t in range(GT):
                    last = dve.tensor_scalar(xn[u][:, t, :], flat(res[:, bass.ds(t0 + t, 1), :]),
                                             mean[:, bass.ds(t0 + t, 1)], rstd[:, bass.ds(t0 + t, 1)],
                                             ALU.subtract, ALU.mult)
                last.then_inc(xn_ready[u], 1)

            def xt_lo(b, u):
                dve.wait_ge(xth_ready[u], b + 1)
                dve.tensor_tensor(xtl[u][:, :], acc[u][:, :], xth[u][:, :].bitcast(F32), ALU.subtract
                                  ).then_inc(xtl_ready[u], 1)

            def hidden(b, u, c):
                g = 2 * b + u
                dve.wait_ge(sg_ready[c], g + 1)
                dve.wait_ge(ffn_done, FIRST + g)
                dve.tensor_tensor(h[c][:, :], sg[c][:, :], big[c][:, GC:2 * GC], ALU.mult).then_inc(h_ready[c], 1)

            def add_shared(b, u):
                g = 2 * b + u
                dve.wait_ge(ffn_done, FIRST + g + 1)
                r = flat(res[:, bass.ds(g * GT, GT), :])
                dve.tensor_tensor(r, acc[u][:, :], r, ALU.add).then_inc(shared_added[u], 1)

            def top_logit(b, u):
                g = 2 * b + u
                dve.wait_ge(vr_kept[u], FIRST + b + 1)
                dve.tensor_reduce(highest[:, bass.ds(g * GT, GT)], vr_all[:, bass.ds(g * GT, GT), KD:VR], AX.X,
                                  ALU.max).then_inc(top_ready, 1)

            def to_score(b, u):
                s = score[:, bass.ds((2 * b + u) * GT, GT)]
                dve.wait_ge(tanh_ready, 2 * b + u + 1)
                dve.tensor_scalar(s, s, 0.5, 0.5, ALU.mult, ALU.add).then_inc(score_ready, 1)

            def choose(b):
                t = bass.ds(b * BT, BT)
                eq, sel, first = rt_eq[:, 0:BT, :], rt_sel[:, 0:BT, :], rt_small[:, 0, 0:BT]
                dve.wait_ge(top_ready, 2 * b + 2)
                dve.tensor_tensor(eq, vr_all[:, t, KD:VR], spread(highest[:, t], NE), ALU.is_equal
                                  ).then_inc(hot_step, 1)
                dve.wait_ge(hot_step, 3 * b + 1)
                dve.tensor_tensor(sel, eq, repeat(lastf[:, :], BT), ALU.mult).then_inc(hot_step, 1)
                dve.wait_ge(hot_step, 3 * b + 2)
                dve.tensor_reduce(first, sel, AX.X, ALU.max).then_inc(hot_step, 1)
                dve.wait_ge(hot_step, 3 * b + 3)
                dve.tensor_tensor(onehot[:, t, :], sel, spread(first, NE), ALU.is_equal).then_inc(onehot_ready, 1)

            def weights_lo(b, k):
                e = EB * b + k
                dve.wait_ge(weh_ready, e + 1)
                dve.tensor_tensor(flat(wel[:, bass.ds(e, 1), :]), flat(we_raw[:, bass.ds(e, 1), :]),
                                  flat(weh[:, bass.ds(e, 1), :]).bitcast(F32), ALU.subtract
                                  ).then_inc(wel_ready, 1)

            dve.wait_ge(x_loaded[0], 16)
            statistics(0)
            dve.wait_ge(ws_loaded, 16)
            dve.tensor_copy(wsh[:, :], ws_raw[:, 0:DOWN0]).then_inc(ws_hi, 1)
            for u in range(2):
                normalize(0, u)
            dve.wait_ge(ws_hi, 1)
            dve.tensor_tensor(wsl[:, :], ws_raw[:, 0:DOWN0], wsh[:, :].bitcast(F32), ALU.subtract
                              ).then_inc(ws_split, 1)
            xt_lo(0, 0)
            dve.wait_ge(x_loaded[1], 16)
            dve.wait_ge(const_made, CONSTS)

            def step(b, more):
                first = isinstance(b, int) and b == 0
                if more:
                    statistics(b + 1)
                if not first:
                    add_shared(b - 1, 1)
                top_logit(b, 0)
                hidden(b, 0, 0)
                to_score(b, 0)
                xt_lo(b, 1)
                hidden(b, 0, 1)
                if more:
                    normalize(b + 1, 0)
                top_logit(b, 1)
                weights_lo(b, 0)
                to_score(b, 1)
                add_shared(b, 0)
                hidden(b, 1, 0)
                weights_lo(b, 1)
                if more:
                    xt_lo(b + 1, 0)
                choose(b)
                weights_lo(b, 2)
                hidden(b, 1, 1)
                if more:
                    normalize(b + 1, 1)
                weights_lo(b, 3)
                if first:
                    for n in range(2, B):
                        dve.wait_ge(x_loaded[n], 16)

            def split_lo(b, half):
                cols = slice(half * S // 2, (half + 1) * S // 2)
                dve.wait_ge(q_hi_ready, 2 * b + half + 1)
                dve.scalar_tensor_tensor(out=q_hl[KD:P, cols], in0=q_raw[KD:P, cols], scalar=float(KD) ** -0.5,
                                         in1=q_hl[KD:P, cols].bitcast(F32), op0=ALU.mult, op1=ALU.subtract
                                         ).then_inc(q_lo_ready, 1)
                dve.wait_ge(k_hi_ready, 2 * b + half + 1)
                dve.tensor_tensor(k_lo[:, cols], k_lo[:, cols].bitcast(F32), k_hi[:, cols].bitcast(F32),
                                  ALU.subtract).then_inc(k_lo_ready, 1)

            def split_first():
                for half in range(2):
                    split_lo(0, half)

            phase_a(dve, step, split_first)
            add_shared(B - 1, 1)

            step_no = [0]

            def done(ins):
                step_no[0] += 1
                ins.then_inc(rt_step, 1)
                dve.wait_ge(rt_step, step_no[0])

            slotf = rt_small[:, 1, 0:NT]
            counts, tiles, upto_tiles, start = (rt_small[:, i, 0:NE] for i in range(2, 6))
            over = rt_small[0:1, 6, 0:NS]

            def routing():
                dve.wait_ge(ranked, 1)
                done(dve.tensor_reduce(counts, mid[1][:, 0:NT * NE].rearrange("p (t e) -> p e t", e=NE), AX.X,
                                       ALU.add))
                done(dve.tensor_scalar(rt_int[:, :], counts, float(P - 1), None, ALU.add))
                done(dve.tensor_scalar(rt_int[:, :], rt_int[:, :], 7, None, ALU.logical_shift_right))
                done(dve.tensor_copy(tiles, rt_int[:, :]))
                done(dve.tensor_tensor(rt_sel[:, 0:NE, :], upto[:, :, :], repeat(tiles, NE), ALU.mult))
                done(dve.tensor_reduce(upto_tiles, rt_sel[:, 0:NE, :], AX.X, ALU.add))
                done(dve.tensor_tensor(start, upto_tiles, tiles, ALU.subtract))
                done(dve.tensor_scalar(start, start, float(P), None, ALU.mult))
                done(dve.tensor_tensor(rt_sel[:, :, :], mid[0][:, 0:NT * NE].rearrange("p (t e) -> p t e", e=NE),
                                       repeat(start, NT), ALU.add))
                done(dve.tensor_tensor(rt_sel[:, :, :], rt_sel[:, :, :], onehot[:, :, :], ALU.mult))
                done(dve.tensor_reduce(slotf, rt_sel[:, :, :], AX.X, ALU.add))
                dve.tensor_copy(slot[:, :], slotf).then_inc(slots_ready, 1)
                done(dve.tensor_tensor(rt_eq[0:1, :, :], spread(slotno[0:1, :], NE),
                                       repeat(upto_tiles[0:1, :], NS), ALU.is_ge))
                done(dve.tensor_reduce(over, rt_eq[0:1, :, :], AX.X, ALU.add))
                done(dve.tensor_scalar(over, over, float(NE - 1), None, ALU.min))
                pairs = over.rearrange("p (n v) -> p n v", v=2)
                done(dve.scalar_tensor_tensor(out=pair_code[:, 2:2 + NP], in0=pairs[:, :, 1], scalar=float(1 << CODE),
                                              in1=pairs[:, :, 0], op0=ALU.mult, op1=ALU.add))
                dve.scalar_tensor_tensor(out=step_experts[:, :], in0=pair_code[:, 0:NP + 2],
                                         scalar=float(1 << 2 * CODE), in1=pair_code[:, 2:NP + 4], op0=ALU.mult,
                                         op1=ALU.add).then_inc(experts_ready, 1)

            def row_max(b, i):
                dve.wait_ge(s_done, FIRST + b * BT + i + 1)
                dve.tensor_reduce(negmax[:, i:i + 1], big[i % 2][:, 0:(i + 1) * P], AX.X, ALU.max,
                                  negate=True).then_inc(max_ready, 1)

            def probs_lo(b, n):
                _, c0 = block_of(n)
                dve.wait_ge(pth_ready, b * STEPS + n + 1)
                dve.wait_ge(pv_done, FIRST + b * STEPS + max(n - 1, 0))
                dve.tensor_tensor(ptl[n % 2][:, c0:GC], mid[n % 2][:, c0:GC],
                                  pth[n % 2][:, c0:GC].bitcast(F32), ALU.subtract).then_inc(ptl_ready, 1)

            def add_attention(b, g):
                dve.wait_ge(exp_done, FIRST + b * BT + (g + 1) * GT)
                dve.reciprocal(rden[:, g * GT:(g + 1) * GT], den[:, g * GT:(g + 1) * GT]
                               ).then_inc(rden_ready[g], 1)
                dve.wait_ge(rden_ready[g], FIRST + b + 1)
                dve.wait_ge(proj_done, FIRST + b * BG + g + 1)
                for t in range(GT):
                    r = flat(res[:, bass.ds(b * BT + g * GT + t, 1), :])
                    last = dve.scalar_tensor_tensor(
                        out=r, in0=acc[g][:, t * P:(t + 1) * P], scalar=rden[:, g * GT + t:g * GT + t + 1],
                        in1=r, op0=ALU.mult, op1=ALU.add)
                last.then_inc(att_added[g], 1)

            def first_half(b, first):
                for i in range(GT):
                    row_max(b, i)
                if first:
                    routing()
                dve.wait_ge(v_hi_ready, b + 1)
                dve.tensor_tensor(v_hl[:, :, KD:2 * KD], v_raw[:, :, :], v_hl[:, :, 0:KD].bitcast(F32),
                                  ALU.subtract).then_inc(v_lo_ready, 1)
                if not first:
                    add_attention(b - 1, 1)
                for n in range(GT):
                    probs_lo(b, n)
                    row_max(b, GT + n)

            def second_half(b, following):
                probs_lo(b, GT)
                add_attention(b, 0)
                for n in range(GT + 1, STEPS):
                    probs_lo(b, n)
                    if following is not None and n in (GT + 2, GT + 4):
                        split_lo(following, (n - GT) // 2 - 1)

            phase_c(dve, first_half, second_half)
            add_attention(B - 1, 1)

            def step(p, q, loop=False):
                if live(p - 1, loop):
                    dve.wait_ge(eht_done, p)
                    dve.wait_ge(ey_done, max(p - 2, 0) if not loop else p - 2)
                    dve.tensor_copy(eht[1 - q][:, :, :, :].rearrange("p v c t -> p (v c t)"), mid[1][:, :]
                                    ).then_inc(eht_ready, 1)
                if live(p, loop):
                    dve.wait_ge(esg_ready, p + 1)
                    dve.tensor_tensor(eh[q][:, :, :], esg[q][:, :, :],
                                      big[q][:, :].rearrange("p (v f) -> p v f", v=2)[:, :, FE:2 * FE],
                                      ALU.mult).then_inc(eh_ready, 1)
                if live(p + 2, loop):
                    rows_lo(p + 2, q)

            def rows_lo(p, q):
                dve.wait_ge(xeh_ready, p + 1)
                dve.tensor_tensor(flat(xel[q][:, :, :]), mid[0][:, 0:2 * P],
                                  flat(xeh[q][:, :, :]).bitcast(F32), ALU.subtract).then_inc(xel_ready, 1)

            for q in range(2):
                rows_lo(q, q)
            phase_d(dve, step)

        @block.scalar
        def _(act):
            def xt_hi(b, u):
                act.wait_ge(xt_done[u], FIRST + b + 1)
                act.wait_ge(gu_done[1], 2 * b + u - 1) if not (isinstance(b, int) and b == 0) else None
                act.copy(xth[u][:, :], acc[u][:, :]).then_inc(xth_ready[u], 1)

            def keep(b, u):
                g = 2 * b + u
                act.wait_ge(vr_done[u], b + 1)
                act.copy(vr_all[:, bass.ds(g * GT, GT), :],
                         mid[0][:, 0:GT * VR].rearrange("p (t n) -> p t n", t=GT)).then_inc(vr_kept[u], 1)
                act.wait_ge(qk_done[u], b + 1)
                act.copy(qk_all[:, bass.ds(g * GC, GC)], mid[1][:, :]).then_inc(qk_kept[u], 1)

            def gate(b, u, c):
                g = 2 * b + u
                act.wait_ge(gu_done[c], g + 1)
                act.wait_ge(h_ready[c], FIRST + g)
                act.activation(sg[c][:, :], big[c][:, 0:GC], ACT.Silu).then_inc(sg_ready[c], 1)

            def score_tanh(b, u):
                t = bass.ds((2 * b + u) * GT, GT)
                act.wait_ge(top_ready, 2 * b + u + 1)
                act.activation(score[:, t], highest[:, t], ACT.Tanh, scale=0.5).then_inc(tanh_ready, 1)

            def weights_hi(b, k):
                e = EB * b + k
                act.copy(flat(weh[:, bass.ds(e, 1), :]), flat(we_raw[:, bass.ds(e, 1), :])).then_inc(weh_ready, 1)

            def step(b, more):
                keep(b, 0)
                score_tanh(b, 0)
                gate(b, 0, 0)
                xt_hi(b, 1)
                gate(b, 0, 1)
                if isinstance(b, int):
                    act.wait_ge(we_loaded[b], 16)
                weights_hi(b, 0)
                keep(b, 1)
                score_tanh(b, 1)
                weights_hi(b, 1)
                gate(b, 1, 0)
                if more:
                    xt_hi(b + 1, 0)
                weights_hi(b, 2)
                gate(b, 1, 1)
                weights_hi(b, 3)
                if isinstance(b, int) and b == 0:
                    for n in range(1, B - 1):
                        act.wait_ge(we_loaded[n], 16)

            def split_hi(b, half):
                cols = slice(half * S // 2, (half + 1) * S // 2)
                act.wait_ge(raw_ready, 80 * b + 80)
                act.wait_ge(s_done, FIRST + b * BT)
                act.mul(q_hl[:, cols], q_raw[:, cols], float(KD) ** -0.5).then_inc(q_hi_ready, 1)
                act.copy(k_hi[:, cols], k_lo[:, cols].bitcast(F32)).then_inc(k_hi_ready, 1)

            def split_first():
                for half in range(2):
                    split_hi(0, half)

            xt_hi(0, 0)
            phase_a(act, step, split_first)

            def exp(b, i):
                act.wait_ge(max_ready, b * BT + i + 1)
                if i >= GT:
                    act.wait_ge(pt_done, FIRST + b * STEPS + i - GT + 1)
                elif not (isinstance(b, int) and b == 0):
                    act.wait_ge(pt_done, FIRST + b * STEPS - GT + i + 1)
                act.wait_ge(rden_ready[i // GT], FIRST + b)
                act.activation(prob[i % GT][:, 0:(i + 1) * P], big[i % 2][:, 0:(i + 1) * P], ACT.Exp,
                               bias=negmax[:, i:i + 1], accum_out=den[:, i:i + 1]).then_inc(exp_done, 1)

            def probs_hi(b, n):
                _, c0 = block_of(n)
                act.wait_ge(pt_done, FIRST + b * STEPS + n + 1)
                act.wait_ge(pv_done, FIRST + b * STEPS + max(n - 1, 0))
                act.copy(pth[n % 2][:, c0:GC], mid[n % 2][:, c0:GC]).then_inc(pth_ready, 1)

            def out_copy(b, g):
                act.wait_ge(pv_done, FIRST + b * STEPS + (STEPS if g else GT))
                act.wait_ge(proj_done, FIRST + b * BG + g)
                act.copy(ot[:, :], acc[g][:, :]).then_inc(ot_ready, 1)

            def first_half(b, first):
                if first:
                    for u in range(2):
                        act.wait_ge(shared_added[u], FIRST + B)
                        act.wait_ge(rows_kept[u], FIRST + B)
                for i in range(GT):
                    exp(b, i)
                act.wait_ge(pv_done, FIRST + b * STEPS)
                act.copy(v_hl[:, :, 0:KD], v_raw[:, :, :]).then_inc(v_hi_ready, 1)
                for n in range(GT):
                    probs_hi(b, n)
                    exp(b, GT + n)
                out_copy(b, 0)

            def second_half(b, following):
                for n in range(GT, STEPS):
                    probs_hi(b, n)
                    if following is not None and n in (GT + 1, GT + 3):
                        split_hi(following, (n - GT) // 2)
                out_copy(b, 1)

            phase_c(act, first_half, second_half)

            def step(p, q, loop=False):
                if live(p - 2, loop):
                    act.wait_ge(ey_done, p - 1)
                    act.wait_ge(y_added[q], 16 * (p - 2 - q))
                    act.copy(flat(y[q][:, :, :]), acc[q][:, 0:2 * P]).then_inc(y_ready, 1)
                if live(p, loop):
                    act.wait_ge(egu_done, 2 * p + 2)
                    act.wait_ge(eh_ready, max(p - 1, 0) if not loop else p - 1)
                    act.activation(esg[q][:, :, :], big[q][:, :].rearrange("p (v f) -> p v f", v=2)[:, :, 0:FE],
                                   ACT.Silu).then_inc(esg_ready, 1)
                if live(p + 2, loop):
                    rows_hi(p + 2, q)

            def rows_hi(p, q):
                act.wait_ge(xet_done, p + 1)
                act.copy(flat(xeh[q][:, :, :]), mid[0][:, 0:2 * P]).then_inc(xeh_ready, 1)

            for q in range(2):
                rows_hi(q, q)
            phase_d(act, step)

        @block.tensor
        def _(pe):
            def product(dst, weights, moving):
                (wh, wl), (mh, ml) = weights, moving
                pe.matmul(dst, wh, mh, start=True, stop=False)
                pe.matmul(dst, wh, ml, start=False, stop=False)
                return pe.matmul(dst, wl, mh, start=False, stop=True)

            def small(a0, a1):
                return wsh[:, a0:a1], wsl[:, a0:a1]

            def transpose_x(b, u):
                pe.wait_ge(xn_ready[u], b + 1)
                pe.wait_ge(shared_added[u], FIRST + b)
                for t in range(GT):
                    last = pe.transpose(acc[u][:, t * P:(t + 1) * P], xn[u][:, t, :], identf[:, :])
                last.then_inc(xt_done[u], 1)

            def project_x(b, u):
                xt = xth[u], xtl[u]
                pe.wait_ge(xtl_ready[u], b + 1)
                pe.wait_ge(vr_kept[1 - u], FIRST + b + u)
                for t in range(GT):
                    cols = slice(t * P, (t + 1) * P)
                    last = product(mid[0][:, t * VR:(t + 1) * VR], (xt[0][:, cols], xt[1][:, cols]),
                                   small(VR0, VR0 + VR))
                last.then_inc(vr_done[u], 1)
                pe.wait_ge(qk_kept[1 - u], FIRST + b + u)
                product(mid[1][:, :], small(QK0, QK0 + P), (xt[0][:, :], xt[1][:, :])).then_inc(qk_done[u], 1)

            def gate_up(b, u, c):
                pe.wait_ge(h_ready[c], FIRST + 2 * b + u)
                for n, w0 in enumerate((GATE0, UP0)):
                    last = product(big[c][:, n * GC:(n + 1) * GC], small(w0 + c * P, w0 + (c + 1) * P),
                                   (xth[u][:, :], xtl[u][:, :]))
                last.then_inc(gu_done[c], 1)

            def down(b, u):
                for c in range(FC):
                    pe.wait_ge(h_ready[c], FIRST + 2 * b + u + 1)
                for t in range(GT):
                    for c in range(FC):
                        cols = slice(t * P, (t + 1) * P)
                        last = pe.matmul(acc[u][:, cols], h[c][:, cols],
                                         ws_raw[:, DOWN0 + c * P:DOWN0 + (c + 1) * P], start=c == 0,
                                         stop=c == FC - 1)
                last.then_inc(ffn_done, 1)

            def step(b, more):
                project_x(b, 0)
                if not (isinstance(b, int) and b == 0):
                    down(b - 1, 1)
                gate_up(b, 0, 0)
                transpose_x(b, 1)
                gate_up(b, 0, 1)
                project_x(b, 1)
                down(b, 0)
                gate_up(b, 1, 0)
                if more:
                    transpose_x(b + 1, 0)
                gate_up(b, 1, 1)

            pe.wait_ge(const_made, 2)
            transpose_x(0, 0)
            pe.wait_ge(ws_split, 1)
            phase_a(pe, step)
            down(B - 1, 1)
            pe.wait_ge(const_made, CONSTS)
            pe.wait_ge(onehot_ready, B)
            oh = flat(onehot[:, :, :])
            pe.matmul(mid[1][:, 0:NT * NE], onesb[:, :], oh, start=True, stop=True)
            pe.matmul(mid[0][:, 0:NT * NE], before[:, :], oh, start=True, stop=True, skip_group_check=True)
            for t in range(1, NT):
                last = pe.matmul(mid[0][:, t * NE:NT * NE], onesb[:, :], oh[:, 0:(NT - t) * NE], start=False,
                                 stop=True, skip_group_check=True)
            last.then_inc(ranked, 1)

            def scores(b, i):
                if i == 0:
                    pe.wait_ge(q_lo_ready, FIRST + 2 * b + 2)
                    pe.wait_ge(k_lo_ready, 2 * b + 2)
                pe.wait_ge(exp_done, FIRST + b * BT + max(i - 1, 0))
                q = q_hl[:, i * P:(i + 1) * P]
                for k0 in range(0, (i + 1) * P, GC):
                    k1 = min(k0 + GC, (i + 1) * P)
                    dst = big[i % 2][:, k0:k1]
                    pe.matmul(dst, q, k_hi[:, k0:k1], start=True, stop=False)
                    if k1 == (i + 1) * P:
                        pe.matmul(big[i % 2][:, i * P:k1], identb[:, :], causal[:, :], start=False, stop=False)
                    last = pe.matmul(dst, q, k_lo[:, k0:k1], start=False, stop=True)
                last.then_inc(s_done, 1)

            def transposes(b, n):
                kb, c0 = block_of(n)
                g = 0 if n < GT else 1
                pe.wait_ge(exp_done, FIRST + b * BT + (g + 1) * GT)
                pe.wait_ge(ptl_ready, FIRST + b * STEPS + max(n - 1, 0))
                for r in range(c0 // P, GT):
                    last = pe.transpose(mid[n % 2][:, r * P:(r + 1) * P], prob[r][:, kb * P:(kb + 1) * P],
                                        identf[:, :])
                last.then_inc(pt_done, 1)

            def weigh(b, n):
                kb, c0 = block_of(n)
                g = 0 if n < GT else 1
                if n == 0:
                    pe.wait_ge(v_lo_ready, FIRST + b + 1)
                if kb == 0:
                    pe.wait_ge(att_added[g], FIRST + b)
                pe.wait_ge(ptl_ready, FIRST + b * STEPS + n + 1)
                pe.matmul(acc[g][:, c0:GC], v_hl[:, kb, :], pth[n % 2][:, c0:GC], start=kb == 0, stop=False,
                          skip_group_check=True)
                pe.matmul(acc[g][:, c0:GC], v_hl[:, kb, :], ptl[n % 2][:, c0:GC], start=False, stop=True,
                          skip_group_check=True).then_inc(pv_done, 1)

            def project(b, g):
                pe.wait_ge(ot_ready, b * BG + g + 1)
                for t in range(GT):
                    cols = slice(t * P, (t + 1) * P)
                    last = pe.matmul(acc[g][:, cols], ot[:, cols], ws_raw[:, V20:V20 + P], start=True, stop=True)
                last.then_inc(proj_done, 1)

            def first_half(b, first):
                if first:
                    scores(b, 0)
                    scores(b, 1)
                for i in range(2, GT):
                    scores(b, i)
                if first:
                    pe.wait_ge(slots_ready, 1)
                transposes(b, 0)
                for n in range(GT):
                    scores(b, GT + n)
                    if n + 1 < GT:
                        transposes(b, n + 1)
                    weigh(b, n)

            def second_half(b, following):
                transposes(b, GT)
                for n in range(GT, STEPS):
                    if n + 1 < STEPS:
                        transposes(b, n + 1)
                    if n == GT:
                        project(b, 0)
                    if n == STEPS - 2 and following is not None:
                        scores(following, 0)
                        scores(following, 1)
                    weigh(b, n)
                project(b, 1)

            phase_c(pe, first_half, second_half)

            def experts(p):
                word = pe.value_load(step_experts[0:1, bass.ds(p, 1)], min_val=0, max_val=(1 << 4 * CODE) - 1)
                e = [pe.snap((word >> n * CODE) & (NE - 1)) for n in range(4)]
                return e[:2], e[2:]

            def transpose_rows(p, q):
                pe.wait_ge(xe_loaded[q], 8 * (p - q) + 16)
                pe.wait_ge(xel_ready, p)
                for v in range(2):
                    last = pe.transpose(mid[0][:, v * P:(v + 1) * P], xe[q][:, v, 0:P], identf[:, :])
                last.then_inc(xet_done, 1)

            def gate_up(p, q, v, e, loop):
                if v == 0:
                    pe.wait_ge(xel_ready, p + 1)
                    pe.wait_ge(eh_ready, p - 1 if loop else max(p - 1, 0))
                w = [flat(m[:, bass.ds(e[v], 1), :]) for m in (weh, wel)]
                product(big[q][:, v * GC:(v + 1) * GC], (xeh[q][:, v, :], xel[q][:, v, :]), w
                        ).then_inc(egu_done, 1)

            def transpose_hidden(p, q):
                pe.wait_ge(eh_ready, p + 1)
                pe.wait_ge(eht_ready, p)
                for v in range(2):
                    for c in range(FC):
                        n = v * FC + c
                        last = pe.transpose(mid[1][:, n * P:(n + 1) * P], eh[q][:, v, c * P:(c + 1) * P],
                                            identf[:, :])
                last.then_inc(eht_done, 1)

            def down(p, q, e):
                pe.wait_ge(eht_ready, p + 1)
                pe.wait_ge(y_ready, p)
                for v in range(2):
                    for c in range(FC):
                        last = pe.matmul(acc[q][:, v * P:(v + 1) * P], eht[q][:, v, c, :],
                                         flat(wed[:, bass.ds(e[v], 1), c * P:(c + 1) * P]), start=c == 0,
                                         stop=c == FC - 1)
                last.then_inc(ey_done, 1)

            def step(p, q, loop=False):
                e, e_before = experts(p)
                if live(p, loop):
                    gate_up(p, q, 0, e, loop)
                if live(p - 2, loop):
                    down(p - 2, q, e_before)
                if live(p, loop):
                    gate_up(p, q, 1, e, loop)
                if live(p - 1, loop):
                    transpose_hidden(p - 1, 1 - q)
                if live(p + 2, loop):
                    transpose_rows(p + 2, q)

            pe.wait_ge(wel_ready, NE)
            pe.wait_ge(wed_loaded, 16)
            pe.wait_ge(experts_ready, 1)
            pe.wait_ge(att_added[1], FIRST + B)
            for q in range(2):
                transpose_rows(q, q)
            phase_d(pe, step)


CONSTS = 11
CODE = 4
AHEAD = 4
FIRST = 1


def block_of(n):
    kb = n if n < GT else n - GT
    return kb, (kb if n < GT else max(kb - GT, 0)) * P


def kernel(L0_attn_x, L0_attn_w_q, L0_attn_w_k, L0_attn_w_v1, L0_attn_w_v2, L0_ffn_w_router,
           L0_ffn_gate_up_proj, L0_ffn_down_proj, L0_ffn_w_gate, L0_ffn_w_up, L0_ffn_w_down):
    import concourse.bacc as bacc
    from concourse.bass_utils import run_bass_kernel_spmd

    x = np.ascontiguousarray(L0_attn_x)
    F = L0_ffn_w_down.shape[1]
    E = L0_ffn_down_proj.shape[0]
    w_down = np.transpose(L0_ffn_w_down).reshape(F // P, P, P).transpose(1, 0, 2).reshape(P, F)
    w_small = np.ascontiguousarray(np.concatenate([
        L0_attn_w_q, L0_attn_w_k, L0_attn_w_v1, np.transpose(L0_ffn_w_router), np.transpose(L0_ffn_w_gate),
        np.transpose(L0_ffn_w_up), w_down, np.concatenate([L0_attn_w_v2, L0_attn_w_v2], axis=0)], axis=1))
    gate_up = np.transpose(L0_ffn_gate_up_proj, (1, 0, 2))
    down = np.reshape(L0_ffn_down_proj, (E, F // P, P, P)).transpose(2, 0, 1, 3).reshape(P, E, F)

    n_tokens = x.shape[0] * x.shape[1]
    slot_tiles = n_tokens // P + E
    nc = bacc.Bacc("TRN2", target_bir_lowering=False, num_devices=1)
    arrays = {"x": x, "w_small": w_small, "w_gate_up": np.ascontiguousarray(gate_up),
              "w_down": np.ascontiguousarray(down)}
    args = [nc.dram_tensor(n, a.shape, F32, kind="ExternalInput").ap() for n, a in arrays.items()]
    scratch = nc.dram_tensor("scratch", (slot_tiles * P, P + 1), F32, kind="Internal").ap()
    out = nc.dram_tensor("out", x.shape, F32, kind="ExternalOutput").ap()
    build(nc, *args, scratch, out)
    return run_bass_kernel_spmd(nc, [arrays], core_ids=[0]).results[0]["out"]
```

```python
from contextlib import ExitStack

import numpy as np

import concourse.bass as bass
import concourse.mybir as mybir
from concourse.alu_op_type import AluOpType as ALU

ACT = mybir.ActivationFunctionType
AX = mybir.AxisListType
F32 = mybir.dt.float32
F32R = mybir.dt.float32r
BF16 = mybir.dt.bfloat16
I32 = mybir.dt.int32
U32 = mybir.dt.uint32
U16 = mybir.dt.uint16

P = 128
GT = 4
GC = GT * P
EPS = 1e-5
MASKED = -3.0e38
NO_TOKEN = 1 << 20


def build(nc, x, w_small, w_gate_up, w_down, scratch, out):
    B, S, EMB = x.shape
    NT = B * S // P
    BT = S // P
    BG = BT // GT
    NE, FE = w_down.shape[1], w_down.shape[2]
    KD = 64
    FC = FE // P
    NS = scratch.shape[0] // P
    NP = NS // 2
    ROW = P + 1
    VR = P + NE
    EB = NE // B
    assert NP % 6 == 0 and NE == 1 << CODE and EMB == P and BG == 2 and FC == 2 and w_gate_up.shape[2] == GC
    V10, QK0 = 0, VR
    GATE0 = QK0 + 2 * KD
    UP0 = GATE0 + FE
    DOWN0 = UP0 + FE
    V20 = DOWN0 + FC * P
    WS = V20 + P
    assert w_small.shape[1] == WS
    STEPS = GT + 2 * GT

    with ExitStack() as ctx:
        top = [(nc.sbuf_base + 31) // 32 * 32]

        def size(shape, dt):
            n = 2 if dt in (BF16, U16) else 4
            for d in shape[1:]:
                n *= d
            return (n + 31) // 32 * 32

        def sb(name, shape, dt=F32):
            t = nc.alloc_sbuf_tensor_at(name, shape, dt, offset=top[0])
            top[0] += size(shape, dt)
            return t

        def overlay(start, parts):
            got = []
            for name, shape, dt in parts:
                got.append(nc.alloc_sbuf_tensor_at(name, shape, dt, offset=start))
                start += size(shape, dt)
            return got, start

        res = sb("res", [P, NT, P])
        rows = sb("rows", [P, NT, ROW])
        qk_all = sb("qk_all", [P, NT * P])
        vr_all = sb("vr_all", [P, NT, VR])
        weh = sb("weh", [P, NE, 2 * FE], F32R)
        we_raw = nc.alloc_sbuf_tensor_at("we_raw", [P, NE, 2 * FE], F32, offset=top[0])
        wel = sb("wel", [P, NE, 2 * FE], F32R)
        wed = sb("wed", [P, NE, FE])
        identf = sb("identf", [P, P])
        identb = sb("identb", [P, P], BF16)
        causal = sb("causal", [P, P], BF16)
        before = sb("before", [P, P], BF16)
        onesb = sb("onesb", [P, P], BF16)
        preference = sb("preference", [P, NE])
        upto = sb("upto", [P, NE, NE])
        slotno = sb("slotno", [P, NS])
        stats = sb("stats", [P, BT, 6])
        total, mean, diff, sq, m2, squares, var, rstd = [sb(f"ln{i}", [P, BT]) for i in range(8)]
        minus_half = sb("minus_half", [P, GT])
        table_use = sb("table_use", [P, 1])
        highest, score = sb("highest", [P, NT]), sb("score", [P, NT])
        onehot = sb("onehot", [P, NT, NE], BF16)
        slot = sb("slot", [P, NT], U32)
        pair_code = sb("pair_code", [1, 2 + NP + 2])
        step_experts = sb("step_experts", [1, NP + 2], U16)
        ids = sb("ids", [P, NS], U32)
        blank = sb("blank", [P, ROW])
        xe = [sb(f"xe{q}", [P, 2, ROW]) for q in range(2)]
        q_raw = sb("q_raw", [P, S])
        q_hl = sb("q_hl", [P, S], F32R)
        k_raw = sb("k_raw", [P, S])
        k_hi, k_lo = sb("k_hi", [P, S], F32R), sb("k_lo", [P, S], F32R)
        negmax, den, rden = sb("negmax", [P, BT]), sb("den", [P, BT]), sb("rden", [P, BT])
        att_start = top[0]
        ws_raw = sb("ws_raw", [P, WS])
        wsh = sb("wsh", [P, DOWN0 - QK0], F32R)
        wsl = sb("wsl", [P, DOWN0 - QK0], F32R)
        a, a_end = overlay(top[0], [(f"xn{u}", [P, GT, P], F32) for u in range(2)]
                           + [(f"xth{u}", [P, GC], F32R) for u in range(2)]
                           + [(f"xtl{u}", [P, GC], F32R) for u in range(2)]
                           + [(f"sg{c}", [P, GC], F32) for c in range(FC)]
                           + [(f"h{c}", [P, GC], F32) for c in range(FC)]
                           + [("hot_eq", [P, BT, NE], F32), ("hot_sel", [P, BT, NE], F32),
                              ("hot_first", [P, BT], F32), ("xt", [P, GC], F32)])
        (xn, xth, xtl, sg, h), (hot_eq, hot_sel, hot_first, xt) = [a[2 * n:2 * n + 2] for n in range(5)], a[10:]
        c, c_end = overlay(att_start, [(f"prob{i}", [P, (i + 1) * P], F32) for i in range(BT)]
                           + [(f"pt{n}", [P, GC], F32) for n in range(2)])
        prob, pt = c[:BT], c[BT:]
        (rt_eq, rt_sel, rt_ranks, rt_small), b_end = overlay(c_end, [
            ("rt_eq", [P, NS, NE], F32), ("rt_sel", [P, NE, NE], F32), ("rt_ranks", [P, NT, NE], F32),
            ("rt_small", [P, 2, NE], F32)])
        rt_counts = rt_eq[:, 0:NT, :]
        d, d_end = overlay(att_start, [(f"xeh{q}", [P, 2, P], F32R) for q in range(2)]
                           + [(f"xel{q}", [P, 2, P], F32R) for q in range(2)]
                           + [(f"esg{q}", [P, 2, FE], F32) for q in range(2)]
                           + [(f"eh{q}", [P, 2, FE], F32) for q in range(2)]
                           + [(f"eht{q}", [P, 2, FC, P], F32) for q in range(2)]
                           + [(f"y{q}", [P, 2, P], F32) for q in range(2)])
        xeh, xel, esg, eh, eht, y = [d[2 * n:2 * n + 2] for n in range(6)]
        assert max(a_end, b_end, d_end) <= nc.sbuf_usable_end, (a_end, b_end, d_end, nc.sbuf_usable_end)

        def psum(name, cols):
            return ctx.enter_context(nc.psum_tensor(name, [P, cols], F32))

        big = [psum(f"big{n}", 2 * GC) for n in range(2)]
        mid = [psum(f"mid{n}", GC) for n in range(2)]
        acc = [psum(f"acc{n}", GC) for n in range(2)]

        def sem(name, n=None):
            if n is None:
                return ctx.enter_context(nc.semaphore(name))
            return [ctx.enter_context(nc.semaphore(f"{name}{i}")) for i in range(n)]

        x_group_loaded = sem("x_group_loaded", 2)
        x_loaded, we_loaded, wed_loaded = sem("x_loaded", B), sem("we_loaded", B), sem("wed_loaded")
        ws_loaded = sem("ws_loaded")
        blanked, scratch_blank = sem("blanked"), sem("scratch_blank")
        const_made, const_step = sem("const_made"), sem("const_step")
        wsl_ready, wsh_ready = sem("wsl_ready"), sem("wsh_ready")
        v12_done, v12_kept = sem("v12_done"), sem("v12_kept")
        ln_step, var_ready, rstd_ready = sem("ln_step"), sem("var_ready"), sem("rstd_ready")
        xn_ready, rows_kept, xt_done = sem("xn_ready", 2), sem("rows_kept", 2), sem("xt_done", 2)
        xt_kept = sem("xt_kept", 2)
        xth_ready, xtl_ready = sem("xth_ready", 2), sem("xtl_ready", 2)
        vr_done, vr_kept = sem("vr_done", 2), sem("vr_kept", 2)
        qk_done, qk_kept = sem("qk_done", 2), sem("qk_kept", 2)
        gu_done, sg_ready, h_ready = sem("gu_done", 2), sem("sg_ready", 2), sem("h_ready", 2)
        ffn_done, shared_added = sem("ffn_done"), sem("shared_added", 2)
        top_ready, tanh_ready, score_ready = sem("top_ready"), sem("tanh_ready"), sem("score_ready")
        hot_step, onehot_ready = sem("hot_step"), sem("onehot_ready")
        weh_ready, wel_ready = sem("weh_ready"), sem("wel_ready")
        rt_step, ranked, ranks_kept = sem("rt_step"), sem("ranked"), sem("ranks_kept")
        slots_ready, experts_ready = sem("slots_ready"), sem("experts_ready")
        row_sent = sem("row_sent")
        raw_ready, q_hi_ready, q_lo_ready = sem("raw_ready"), sem("q_hi_ready"), sem("q_lo_ready")
        k_hi_ready, k_lo_ready = sem("k_hi_ready"), sem("k_lo_ready")
        s_done, max_ready, exp_done = sem("s_done"), sem("max_ready"), sem("exp_done")
        pt_done, pt_ready, pv_done = sem("pt_done"), sem("pt_ready"), sem("pv_done")
        rden_ready, att_added, out_written = sem("rden_ready"), sem("att_added", 2), sem("out_written")
        xe_loaded, ids_kept = sem("xe_loaded", 2), sem("ids_kept")
        xet_done, xeh_ready, xel_ready = sem("xet_done"), sem("xeh_ready"), sem("xel_ready")
        egu_done, esg_ready, eh_ready = sem("egu_done"), sem("esg_ready"), sem("eh_ready")
        eht_done, eht_ready = sem("eht_done"), sem("eht_ready")
        ey_done, y_ready, y_added = sem("ey_done"), sem("y_ready"), sem("y_added", 2)

        primed = [ffn_done, *xt_done, *rows_kept, *h_ready, *shared_added, *vr_kept, *qk_kept, s_done, k_lo_ready,
                  pv_done, pt_done, rden_ready, exp_done, pt_ready, *att_added]
        out_rows = out.rearrange("b s e -> (b s) e")
        out_tiles = out_rows.rearrange("(t p) e -> p t e", p=P)
        x_tiles = x.rearrange("b (t p) e -> p (b t) e", p=P)
        block = ctx.enter_context(nc.Block())

        def flat(ap):
            return ap.rearrange("p a b -> p (a b)")

        def spread(ap, n):
            return ap[:, :, None].to_broadcast([ap.shape[0], ap.shape[1], n])

        def repeat(ap, n):
            return ap[:, None, :].to_broadcast([ap.shape[0], n, ap.shape[1]])

        def phase_a(eng, step):
            step(0, True)
            with eng.Fori(1, B - 1) as b:
                step(b, True)
            step(B - 1, False)

        def phase_c(eng, first_half, second_half, routing=None):
            first_half(0, True)
            if routing:
                routing()
            with eng.Fori(1, B) as b:
                second_half(b - 1, b)
                first_half(b, False)
            second_half(B - 1, None)

        def phase_d(eng, step):
            for p in range(4):
                step(p, p % 2)
            with eng.Fori(0, (NP - 6) // 6) as i:
                for k in range(6):
                    step(6 * i + 4 + k, k % 2, True)
            for p in range(NP - 2, NP + 2):
                step(p, p % 2)

        def live(p, loop):
            return loop or 0 <= p < NP

        def used(p):
            return 1 if isinstance(p, int) and p == NP - 1 else 2

        @block.sync
        def _(sp):
            def load_x(b):
                sp.dma_start(res[:, b * BT:(b + 1) * BT, :], x_tiles[:, b * BT:(b + 1) * BT, :]
                             ).then_inc(x_loaded[b], 16)

            def load_x_group(u):
                t = slice(u * GT, (u + 1) * GT)
                sp.dma_start(res[:, t, :], x_tiles[:, t, :]).then_inc(x_group_loaded[u], 16)

            for u in range(2):
                load_x_group(u)
            sp.dma_start(ws_raw[:, :], w_small).then_inc(ws_loaded, 16)
            load_x(1)
            for b in range(B):
                if b >= 2:
                    load_x(b)
                e = slice(b * EB, (b + 1) * EB)
                sp.dma_start(we_raw[:, e, :], w_gate_up[:, e, :]).then_inc(we_loaded[b], 16)
            sp.wait_ge(blanked, 2)
            sp.dma_start(scratch.rearrange("(t p) r -> p t r", p=P),
                         blank[:, None, :].to_broadcast([P, NS, ROW])).then_inc(scratch_blank, 16)
            sp.dma_start(wed[:, :, :], w_down).then_inc(wed_loaded, 16)

            def load_raw(col):
                for half in range(2):
                    at_half = slice(half * KD, (half + 1) * KD)
                    sp.dma_start(q_raw[at_half, :], qk_all[0:KD, bass.ds(col, S)]).then_inc(raw_ready, 16)
                    sp.dma_start(k_raw[at_half, :], qk_all[KD:P, bass.ds(col, S)]
                                 ).then_inc(raw_ready, 16)

            def store(t):
                sp.dma_start(out_tiles[:, bass.ds(t, GT), :], res[:, bass.ds(t, GT), :]).then_inc(out_written, 16)

            for u in range(2):
                sp.wait_ge(qk_kept[u], FIRST + 1)
            load_raw(0)
            for u in range(2):
                sp.wait_ge(qk_kept[u], FIRST + B)
            sp.wait_ge(q_lo_ready, 2)
            sp.wait_ge(k_lo_ready, FIRST + 2)
            load_raw(S)
            with sp.Fori(1, B - 1) as b:
                col = sp.snap((b + 1) * S)
                out_tile = [sp.snap((b - 1) * BT + g * GT) for g in range(BG)]
                sp.wait_ge(att_added[0], FIRST + b)
                store(out_tile[0])
                sp.wait_ge(k_lo_ready, FIRST + 2 * b + 2)
                load_raw(col)
                sp.wait_ge(att_added[1], FIRST + b)
                store(out_tile[1])
            for g in range(BG):
                sp.wait_ge(att_added[g], FIRST + B - 1)
                store((B - 2) * BT + g * GT)

            sp.wait_ge(row_sent, 16 * NT)

            def load_rows(first_slot, q):
                sp.dma_start(xe[q][:, :, :],
                             scratch[bass.ds(first_slot, 2 * P), :].rearrange("(v p) r -> p v r", p=P)
                             ).then_inc(xe_loaded[q], 16)

            def store_last(g):
                sp.wait_ge(att_added[g], FIRST + B)
                store((B - 1) * BT + g * GT)

            for p in range(4):
                if p >= 2:
                    sp.wait_ge(xet_done, p - 1)
                    sp.wait_ge(ids_kept, p - 1)
                load_rows(p * 2 * P, p % 2)
                if p == 1:
                    store_last(0)
            store_last(1)
            with sp.Fori(2, NP // 2) as i:
                first_slot = [sp.snap((2 * i + q) * 2 * P) for q in range(2)]
                used = [sp.snap(2 * i + q - 1) for q in range(2)]
                for q in range(2):
                    sp.wait_ge(xet_done, used[q])
                    sp.wait_ge(ids_kept, used[q])
                    load_rows(first_slot[q], q)
            sp.wait_ge(out_written, 16 * B * BG)
            sp.wait_ge(scratch_blank, 16)
            for q in range(2):
                sp.wait_ge(y_added[q], 16 * (NP - q))

        @block.gpsimd
        def _(pool):
            for s in primed:
                pool.sem_inc(s, FIRST)
            pool.memset(identf[:, :], 0.0).then_inc(const_step, 1)
            pool.memset(minus_half[:, :], -0.5).then_inc(const_made, 1)
            pool.wait_ge(const_step, 1)
            pool.affine_select(out=identf[:, :], in_=identf[:, :], compare_op=ALU.not_equal, fill=1.0, base=0,
                               pattern=[[-1, P]], channel_multiplier=1).then_inc(const_made, 1)

            def rsqrt(b, u):
                first_batch = isinstance(b, int) and b == 0
                t = slice(u * GT, (u + 1) * GT)
                if first_batch or u == 0:
                    pool.wait_ge(var_ready, u + 1 if first_batch else b + 2)
                pool.tensor_tensor(rstd[:, t], var[:, t], minus_half[:, :], ALU.pow).then_inc(rstd_ready, 1)

            pool.wait_ge(const_made, 2)
            rsqrt(0, 0)
            pool.memset(blank[:, 0:P], 0.0).then_inc(blanked, 1)
            pool.memset(pair_code[:, :], 0.0).then_inc(const_made, 1)
            pool.memset(blank[:, P:ROW].bitcast(I32), NO_TOKEN).then_inc(blanked, 1)
            rsqrt(0, 1)
            pool.memset(identb[:, :], 0.0).then_inc(const_step, 1)
            pool.memset(causal[:, :], 0.0).then_inc(const_step, 1)
            pool.memset(before[:, :], 1.0).then_inc(const_step, 1)
            pool.memset(upto[:, :, :], 1.0).then_inc(const_step, 1)
            pool.memset(onesb[:, :], 1.0).then_inc(const_made, 1)
            pool.wait_ge(const_step, 5)
            pool.affine_select(out=identb[:, :], in_=identb[:, :], compare_op=ALU.not_equal, fill=1.0, base=0,
                               pattern=[[-1, P]], channel_multiplier=1).then_inc(const_made, 1)
            pool.affine_select(out=causal[:, :], in_=causal[:, :], compare_op=ALU.is_ge, fill=MASKED, base=0,
                               pattern=[[-1, P]], channel_multiplier=1).then_inc(const_made, 1)
            pool.affine_select(out=before[:, :], in_=before[:, :], compare_op=ALU.is_gt, fill=0.0, base=0,
                               pattern=[[1, P]], channel_multiplier=-1).then_inc(const_made, 1)
            pool.affine_select(out=upto[:, :, :], in_=upto[:, :, :], compare_op=ALU.is_ge, fill=0.0, base=0,
                               pattern=[[1, NE], [-1, NE]], channel_multiplier=0).then_inc(const_made, 1)
            pool.iota(preference[:, :], pattern=[[-1, NE]], base=NE, channel_multiplier=0,
                      allow_small_or_imprecise_dtypes=True).then_inc(const_made, 1)
            pool.iota(slotno[:, :], pattern=[[1, NS]], base=0, channel_multiplier=0,
                      allow_small_or_imprecise_dtypes=True).then_inc(const_made, 1)
            pool.iota(rows[:, :, P].bitcast(I32), pattern=[[P, NT]], base=0, channel_multiplier=1
                      ).then_inc(const_made, 1)

            def scaled_rows(b, u):
                t = bass.ds((2 * b + u) * GT, GT)
                pool.wait_ge(score_ready, 2 * b + u + 1)
                pool.tensor_tensor(rows[:, t, 0:P], xn[u][:, :, :], spread(score[:, t], P), ALU.mult
                                   ).then_inc(rows_kept[u], 1)

            def weights_lo(b, k):
                e = EB * b + k
                pool.wait_ge(weh_ready, e + 1)
                pool.tensor_tensor(flat(wel[:, bass.ds(e, 1), :]), flat(we_raw[:, bass.ds(e, 1), :]),
                                   flat(weh[:, bass.ds(e, 1), :]).bitcast(F32), ALU.subtract
                                   ).then_inc(wel_ready, 1)

            def step(b, more):
                scaled_rows(b, 0)
                if more:
                    for u in range(2):
                        rsqrt(b + 1, u)
                weights_lo(b, 0)
                scaled_rows(b, 1)
                for k in range(1, EB):
                    weights_lo(b, k)

            phase_a(pool, step)

            step_no = [0]

            def done(ins):
                step_no[0] += 1
                ins.then_inc(rt_step, 1)
                pool.wait_ge(rt_step, step_no[0])

            def sum_to_first(part, n):
                while n > 1:
                    n //= 2
                    done(pool.tensor_tensor(part(0, n), part(0, n), part(n, 2 * n), ALU.add))

            def sums_up_to(tiles_counts):
                s = 1
                while s < NT:
                    v = tiles_counts.rearrange("p (k s) e -> p k s e", s=2 * s)
                    done(pool.tensor_tensor(v[:, :, 2 * s - 1, :], v[:, :, 2 * s - 1, :], v[:, :, s - 1, :], ALU.add))
                    s *= 2
                s //= 4
                while s:
                    v = tiles_counts.rearrange("p (k s) e -> p k s e", s=2 * s)
                    done(pool.tensor_tensor(v[:, 1:, s - 1, :], v[:, 1:, s - 1, :], v[:, :-1, 2 * s - 1, :], ALU.add))
                    s //= 2

            counts, upto_tiles, over = rt_counts[:, NT - 1, :], rt_sel[:, :, 0], rt_eq[0:1, :, 0]
            tiles, start = (rt_small[:, i, :] for i in range(2))

            pool.wait_ge(ranks_kept, 2)
            sums_up_to(rt_counts)
            done(pool.tensor_scalar(tiles, counts, 1.0 / P, 0.5 - 0.5 / P, ALU.mult, ALU.add))
            done(pool.tensor_scalar(tiles, tiles, ROUND, None, ALU.add))
            done(pool.tensor_scalar(tiles, tiles, -ROUND, None, ALU.add))
            done(pool.tensor_tensor(rt_sel[:, :, :], upto[:, :, :], repeat(tiles, NE), ALU.mult))
            sum_to_first(lambda a, b: rt_sel[:, :, a:b], NE)
            done(pool.tensor_tensor(start, upto_tiles, tiles, ALU.subtract))
            done(pool.tensor_scalar(start, start, float(P), None, ALU.mult))
            done(pool.tensor_tensor(rt_ranks[:, 1:, :], rt_ranks[:, 1:, :], rt_counts[:, :-1, :], ALU.add))
            done(pool.tensor_tensor(rt_ranks[:, :, :], rt_ranks[:, :, :], repeat(start, NT), ALU.add))
            done(pool.tensor_tensor(rt_ranks[:, :, :], rt_ranks[:, :, :], onehot[:, :, :], ALU.mult))
            sum_to_first(lambda a, b: rt_ranks[:, :, a:b], NE)
            pool.tensor_copy(slot[:, :], rt_ranks[:, :, 0]).then_inc(slots_ready, 1)
            done(pool.tensor_tensor(rt_eq[0:1, :, :], spread(slotno[0:1, :], NE), repeat(upto_tiles[0:1, :], NS),
                                    ALU.subtract))
            done(pool.tensor_scalar(rt_eq[0:1, :, :], rt_eq[0:1, :, :], 0.0, None, ALU.is_ge))
            sum_to_first(lambda a, b: rt_eq[0:1, :, a:b], NE)
            done(pool.tensor_scalar(over, over, float(NE - 1), None, ALU.min))
            pairs = over.rearrange("p (n v) -> p n v", v=2)
            code = pair_code[:, 2:2 + NP]
            done(pool.tensor_scalar(code, pairs[:, :, 1], float(1 << CODE), None, ALU.mult))
            done(pool.tensor_tensor(code, code, pairs[:, :, 0], ALU.add))
            both = rt_eq[0:1, 0:NP + 2, 1]
            done(pool.tensor_scalar(both, pair_code[:, 0:NP + 2], float(1 << 2 * CODE), None, ALU.mult))
            done(pool.tensor_tensor(both, both, pair_code[:, 2:NP + 4], ALU.add))
            pool.tensor_copy(step_experts[:, :], both).then_inc(experts_ready, 1)

            pool.wait_ge(slots_ready, 1)
            pool.wait_ge(scratch_blank, 16)
            for u in range(2):
                pool.wait_ge(rows_kept[u], FIRST + B)
            for t in range(NT):
                pool.indirect_dma_start(scratch, bass.IndirectOffsetOnAxis(ap=slot[:, t:t + 1], axis=0),
                                        rows[:, t, :], None).then_inc(row_sent, 16)
            for p in range(-AHEAD, NP):
                if p + AHEAD < NP:
                    load = p + AHEAD
                    pool.wait_ge(xe_loaded[load % 2], 16 * (load // 2 + 1))
                    pool.tensor_copy(ids[:, 2 * load:2 * load + 2], xe[load % 2][:, :, P].bitcast(U32)
                                     ).then_inc(ids_kept, 1)
                if p == 0:
                    pool.wait_ge(out_written, 16 * B * BG)
                if p >= 0:
                    pool.wait_ge(ids_kept, p + 1)
                    pool.wait_ge(y_ready, p + 1)
                    for t in range(2 * p, 2 * p + used(p)):
                        pool.indirect_dma_start(out_rows, bass.IndirectOffsetOnAxis(ap=ids[:, t:t + 1], axis=0),
                                                y[p % 2][:, t % 2, :], None, bounds_check=NT * P - 1,
                                                oob_is_err=False, compute_op=ALU.add
                                                ).then_inc(y_added[p % 2], 16)

        @block.vector
        def _(dve):
            mean_e, m2_e, mean_o, m2_o = (stats[:, :, i] for i in (1, 2, 4, 5))

            def ln_tiles(b, u):
                if u is None:
                    return slice(0, BT), b * (BT + 6) + 6
                return slice(u * GT, (u + 1) * GT), u * (GT + 6)

            def statistics(b, tiles):
                if not (isinstance(b, int) and b == 0):
                    dve.wait_ge(rstd_ready, 2 * b)
                for t in tiles:
                    dve.bn_stats(stats[:, t, :], flat(res[:, bass.ds(b * BT + t, 1), :])
                                 ).then_inc(ln_step, 1)

            def sum_halves(b, u=None):
                t, n0 = ln_tiles(b, u)
                dve.wait_ge(ln_step, n0 + (BT if u is None else GT))
                dve.tensor_tensor(total[:, t], mean_e[:, t], mean_o[:, t], ALU.add).then_inc(ln_step, 1)
                dve.tensor_tensor(diff[:, t], mean_e[:, t], mean_o[:, t], ALU.subtract).then_inc(ln_step, 1)
                dve.tensor_tensor(m2[:, t], m2_e[:, t], m2_o[:, t], ALU.add).then_inc(ln_step, 1)

            def mean_of_halves(b, u=None):
                t, n0 = ln_tiles(b, u)
                dve.wait_ge(ln_step, n0 + (BT if u is None else GT) + 3)
                if u is None:
                    dve.wait_ge(xn_ready[1], b * GT)
                dve.tensor_scalar(mean[:, t], total[:, t], 0.5, None, ALU.mult).then_inc(ln_step, 1)
                dve.tensor_tensor(sq[:, t], diff[:, t], diff[:, t], ALU.mult).then_inc(ln_step, 1)

            def square_sum(b, u=None):
                t, n0 = ln_tiles(b, u)
                dve.wait_ge(ln_step, n0 + (BT if u is None else GT) + 5)
                dve.scalar_tensor_tensor(out=squares[:, t], in0=sq[:, t], scalar=P / 4, in1=m2[:, t], op0=ALU.mult,
                                         op1=ALU.add).then_inc(ln_step, 1)

            def variance(b, u=None):
                t, n0 = ln_tiles(b, u)
                dve.wait_ge(ln_step, n0 + (BT if u is None else GT) + 6)
                dve.tensor_scalar(var[:, t], squares[:, t], 1.0 / P, EPS, ALU.mult, ALU.add).then_inc(var_ready, 1)

            def normalize(b, u):
                t0 = (2 * b + u) * GT
                dve.wait_ge(xt_done[u], FIRST + b)
                dve.wait_ge(rows_kept[u], FIRST + b)
                dve.wait_ge(rstd_ready, 2 * b + u + 1)
                for t in range(GT):
                    dve.tensor_scalar(xn[u][:, t, :], flat(res[:, bass.ds(t0 + t, 1), :]),
                                      mean[:, u * GT + t:u * GT + t + 1], rstd[:, u * GT + t:u * GT + t + 1],
                                      ALU.subtract, ALU.mult).then_inc(xn_ready[u], 1)

            def xt_lo(b, u):
                dve.wait_ge(xth_ready[u], b + 1)
                dve.tensor_tensor(xtl[u][:, :], xt[:, :], xth[u][:, :].bitcast(F32), ALU.subtract
                                  ).then_inc(xtl_ready[u], 1)

            def hidden(b, u, c):
                g = 2 * b + u
                dve.wait_ge(sg_ready[c], g + 1)
                dve.wait_ge(ffn_done, FIRST + g)
                dve.tensor_tensor(h[c][:, :], sg[c][:, :], big[c][:, GC:2 * GC], ALU.mult).then_inc(h_ready[c], 1)

            def add_shared(b, u):
                g = 2 * b + u
                dve.wait_ge(ffn_done, FIRST + g + 1)
                r = flat(res[:, bass.ds(g * GT, GT), :])
                dve.tensor_tensor(r, acc[u][:, :], r, ALU.add).then_inc(shared_added[u], 1)

            def top_logit(b, u):
                g = 2 * b + u
                dve.wait_ge(vr_kept[u], FIRST + 2 * b + 2)
                dve.tensor_reduce(highest[:, bass.ds(g * GT, GT)], vr_all[:, bass.ds(g * GT, GT), P:VR], AX.X,
                                  ALU.max).then_inc(top_ready, 1)

            def to_score(b, u):
                s = score[:, bass.ds((2 * b + u) * GT, GT)]
                dve.wait_ge(tanh_ready, 2 * b + u + 1)
                dve.tensor_scalar(s, s, 0.5, 0.5, ALU.mult, ALU.add).then_inc(score_ready, 1)

            def choose(b, part):
                t = bass.ds(b * BT, BT)
                eq, sel, first = hot_eq[:, :, :], hot_sel[:, :, :], hot_first[:, :]
                if part == 0:
                    dve.wait_ge(top_ready, 2 * b + 2)
                    dve.tensor_tensor(eq, vr_all[:, t, P:VR], spread(highest[:, t], NE), ALU.is_equal
                                      ).then_inc(hot_step, 1)
                if part == 1:
                    dve.wait_ge(hot_step, 3 * b + 1)
                    dve.tensor_tensor(sel, eq, repeat(preference[:, :], BT), ALU.mult).then_inc(hot_step, 1)
                if part == 2:
                    dve.wait_ge(hot_step, 3 * b + 2)
                    dve.tensor_reduce(first, sel, AX.X, ALU.max).then_inc(hot_step, 1)
                if part == 3:
                    dve.wait_ge(hot_step, 3 * b + 3)
                    dve.tensor_tensor(onehot[:, t, :], sel, spread(first, NE), ALU.is_equal
                                      ).then_inc(onehot_ready, 1)

            def group_statistics(u):
                dve.wait_ge(x_group_loaded[u], 16)
                statistics(0, range(u * GT, (u + 1) * GT))
                for part in (sum_halves, mean_of_halves, square_sum, variance):
                    part(0, u)

            for u in range(2):
                group_statistics(u)
            normalize(0, 0)
            dve.wait_ge(wsh_ready, 1)
            dve.tensor_tensor(wsl[:, :], ws_raw[:, QK0:DOWN0], wsh[:, :].bitcast(F32), ALU.subtract
                              ).then_inc(wsl_ready, 1)
            xt_lo(0, 0)
            dve.wait_ge(x_loaded[1], 16)
            dve.wait_ge(const_made, CONSTS)

            def step(b, more):
                if not (isinstance(b, int) and b == 0):
                    add_shared(b - 1, 1)
                else:
                    normalize(0, 1)
                top_logit(b, 0)
                if more:
                    statistics(b + 1, range(BT // 2))
                hidden(b, 0, 0)
                if more:
                    statistics(b + 1, range(BT // 2, BT - 2))
                xt_lo(b, 1)
                to_score(b, 0)
                hidden(b, 0, 1)
                if more:
                    statistics(b + 1, range(BT - 2, BT))
                    for part in (sum_halves, mean_of_halves, square_sum, variance):
                        part(b + 1)
                top_logit(b, 1)
                if not more:
                    split_q_lo(0, 0)
                    split_k(0, 0)
                add_shared(b, 0)
                to_score(b, 1)
                if more:
                    normalize(b + 1, 0)
                choose(b, 0)
                hidden(b, 1, 0)
                choose(b, 1)
                if more:
                    xt_lo(b + 1, 0)
                choose(b, 2)
                if more:
                    hidden(b, 1, 1)
                    choose(b, 3)
                else:
                    choose(b, 3)
                    hidden(b, 1, 1)
                if more:
                    normalize(b + 1, 1)
                if isinstance(b, int) and b == 0:
                    for n in range(2, B):
                        dve.wait_ge(x_loaded[n], 16)

            def split_q_lo(b, half):
                cols = slice(half * S // 2, (half + 1) * S // 2)
                dve.wait_ge(q_hi_ready, 2 * b + half + 1)
                dve.scalar_tensor_tensor(out=q_hl[KD:P, cols], in0=q_raw[KD:P, cols], scalar=float(KD) ** -0.5,
                                         in1=q_hl[KD:P, cols].bitcast(F32), op0=ALU.mult, op1=ALU.subtract
                                         ).then_inc(q_lo_ready, 1)

            def split_k(b, half):
                cols = slice(half * S // 2, (half + 1) * S // 2)
                dve.wait_ge(raw_ready, 64 * b + 64)
                dve.wait_ge(s_done, FIRST + b * BT)
                dve.tensor_copy(k_hi[:, cols], k_raw[:, cols]).then_inc(k_hi_ready, 1)
                dve.wait_ge(k_hi_ready, 2 * b + half + 1)
                dve.tensor_tensor(k_lo[:, cols], k_raw[:, cols], k_hi[:, cols].bitcast(F32), ALU.subtract
                                  ).then_inc(k_lo_ready, 1)

            phase_a(dve, step)

            def row_max(b, i):
                dve.wait_ge(s_done, FIRST + b * BT + i + 1)
                dve.tensor_reduce(negmax[:, i:i + 1], big[i % 2][:, 0:(i + 1) * P], AX.X, ALU.max,
                                  negate=True).then_inc(max_ready, 1)

            def sums(b):
                dve.wait_ge(exp_done, FIRST + b * BT + BT)
                for g in range(BG):
                    dve.wait_ge(att_added[g], FIRST + b)
                dve.reciprocal(rden[:, :], den[:, :]).then_inc(rden_ready, 1)

            def add_attention(b, g):
                dve.wait_ge(rden_ready, FIRST + b + 1)
                dve.wait_ge(pv_done, FIRST + b * STEPS + (STEPS if g else GT))
                for t in range(GT):
                    r = flat(res[:, bass.ds(b * BT + g * GT + t, 1), :])
                    last = dve.scalar_tensor_tensor(
                        out=r, in0=acc[g][:, t * P:(t + 1) * P], scalar=rden[:, g * GT + t:g * GT + t + 1],
                        in1=r, op0=ALU.mult, op1=ALU.add)
                last.then_inc(att_added[g], 1)

            def first_half(b, first):
                if first:
                    for i in range(BT - 2):
                        row_max(b, i)
                        if i == 1:
                            split_k(0, 1)
                            split_q_lo(0, 1)
                            add_shared(B - 1, 1)
                row_max(b, BT - 2)
                row_max(b, BT - 1)
                if not first:
                    add_attention(b - 1, 1)

            def second_half(b, following):
                sums(b)
                if following is None:
                    add_attention(b, 0)
                    return
                split_k(following, 0)
                split_q_lo(following, 0)
                add_attention(b, 0)
                row_max(following, 0)
                split_q_lo(following, 1)
                row_max(following, 1)
                split_k(following, 1)
                for i in range(2, BT - 2):
                    row_max(following, i)

            phase_c(dve, first_half, second_half)

            def step(p, q, loop=False):
                if live(p - 1, loop):
                    dve.wait_ge(eht_done, p)
                    dve.wait_ge(ey_done, max(p - 2, 0) if not loop else p - 2)
                    n = used(p - 1)
                    dve.tensor_copy(eht[1 - q][:, 0:n, :, :].rearrange("p v c t -> p (v c t)"),
                                    mid[1][:, 0:n * FC * P]).then_inc(eht_ready, 1)
                if live(p, loop):
                    dve.wait_ge(esg_ready, p + 1)
                    n = used(p)
                    dve.tensor_tensor(eh[q][:, 0:n, :], esg[q][:, 0:n, :],
                                      big[q][:, :].rearrange("p (v f) -> p v f", v=2)[:, 0:n, FE:2 * FE],
                                      ALU.mult).then_inc(eh_ready, 1)
                if live(p + 2, loop):
                    rows_lo(p + 2, q)

            def rows_lo(p, q):
                dve.wait_ge(xeh_ready, p + 1)
                n = used(p)
                dve.tensor_tensor(flat(xel[q][:, 0:n, :]), mid[0][:, 0:n * P],
                                  flat(xeh[q][:, 0:n, :]).bitcast(F32), ALU.subtract).then_inc(xel_ready, 1)

            rows_lo(0, 0)
            add_attention(B - 1, 1)
            rows_lo(1, 1)
            phase_d(dve, step)

        @block.scalar
        def _(act):
            def keep_xt(b, u):
                act.wait_ge(xt_done[u], FIRST + b + 1)
                if not (isinstance(b, int) and b == 0 and u == 0):
                    act.wait_ge(vr_done[1 - u], b + u)
                    act.wait_ge(xtl_ready[1 - u], b + u)
                act.copy(xt[:, :], acc[u][:, :]).then_inc(xt_kept[u], 1)
                act.wait_ge(xt_kept[u], b + 1)
                if not (isinstance(b, int) and b == 0):
                    act.wait_ge(gu_done[1], 2 * b + u - 1)
                act.copy(xth[u][:, :], xt[:, :]).then_inc(xth_ready[u], 1)

            def keep(b, u):
                g = 2 * b + u
                act.wait_ge(vr_done[u], b + 1)
                act.copy(vr_all[:, bass.ds(g * GT, GT - 1), :],
                         mid[0][:, 0:(GT - 1) * VR].rearrange("p (t n) -> p t n", n=VR)).then_inc(vr_kept[u], 1)
                act.copy(flat(vr_all[:, bass.ds(g * GT + GT - 1, 1), :]), acc[u][:, 0:VR]).then_inc(vr_kept[u], 1)
                act.wait_ge(qk_done[u], b + 1)
                act.copy(qk_all[:, bass.ds(g * GC, GC)], mid[1][:, :]).then_inc(qk_kept[u], 1)

            def gate(b, u, c):
                g = 2 * b + u
                act.wait_ge(gu_done[c], g + 1)
                act.wait_ge(h_ready[c], FIRST + g)
                act.activation(sg[c][:, :], big[c][:, 0:GC], ACT.Silu).then_inc(sg_ready[c], 1)

            def score_tanh(b, u):
                t = bass.ds((2 * b + u) * GT, GT)
                act.wait_ge(top_ready, 2 * b + u + 1)
                act.activation(score[:, t], highest[:, t], ACT.Tanh, scale=0.5).then_inc(tanh_ready, 1)

            def weights_hi(b, k):
                e = EB * b + k
                act.copy(flat(weh[:, bass.ds(e, 1), :]), flat(we_raw[:, bass.ds(e, 1), :])).then_inc(weh_ready, 1)

            def step(b, more):
                keep(b, 0)
                score_tanh(b, 0)
                gate(b, 0, 0)
                keep_xt(b, 1)
                gate(b, 0, 1)
                if not more:
                    split_q_hi(0, 0)
                if isinstance(b, int):
                    act.wait_ge(we_loaded[b], 16)
                weights_hi(b, 0)
                keep(b, 1)
                score_tanh(b, 1)
                weights_hi(b, 1)
                gate(b, 1, 0)
                if more:
                    keep_xt(b + 1, 0)
                weights_hi(b, 2)
                gate(b, 1, 1)
                if more:
                    weights_hi(b, 3)
                if isinstance(b, int) and b == 0:
                    for n in range(1, B - 1):
                        act.wait_ge(we_loaded[n], 16)

            def split_q_hi(b, half):
                cols = slice(half * S // 2, (half + 1) * S // 2)
                act.wait_ge(raw_ready, 64 * b + 64)
                act.wait_ge(s_done, FIRST + b * BT)
                act.mul(q_hl[:, cols], q_raw[:, cols], float(KD) ** -0.5).then_inc(q_hi_ready, 1)

            def load_table(function):
                act.activation(table_use[:, :], minus_half[:, 0:1], function)

            act.wait_ge(const_made, 1)
            load_table(ACT.Silu)
            act.wait_ge(ws_loaded, 16)
            act.copy(wsh[:, :], ws_raw[:, QK0:DOWN0]).then_inc(wsh_ready, 1)
            act.wait_ge(v12_done, 1)
            act.copy(ws_raw[:, V10:V10 + P], mid[1][:, 0:P]).then_inc(v12_kept, 1)
            keep_xt(0, 0)
            phase_a(act, step)

            def exp(b, i):
                act.wait_ge(max_ready, b * BT + i + 1)
                if not (isinstance(b, int) and b == 0):
                    act.wait_ge(pt_done, FIRST + (b - 1) * STEPS + (i if i < GT else GT + i) + 1)
                act.wait_ge(rden_ready, FIRST + b)
                act.activation(prob[i][:, 0:(i + 1) * P], big[i % 2][:, 0:(i + 1) * P], ACT.Exp,
                               bias=negmax[:, i:i + 1], accum_out=den[:, i:i + 1]).then_inc(exp_done, 1)

            def keep_pt(b, n):
                _, c0 = block_of(n)
                act.wait_ge(pt_done, FIRST + b * STEPS + n + 1)
                act.wait_ge(pv_done, FIRST + b * STEPS + max(n - 1, 0))
                act.copy(pt[n % 2][:, c0:GC], mid[n % 2][:, c0:GC]).then_inc(pt_ready, 1)

            def first_half(b, first):
                if first:
                    for i in range(2):
                        exp(b, i)
                    split_q_hi(0, 1)
                    exp(b, 2)
                    for u in range(2):
                        act.wait_ge(shared_added[u], FIRST + B)
                        act.wait_ge(rows_kept[u], FIRST + B)
                    for n in range(2):
                        act.wait_ge(ranked, 1)
                        act.copy(flat((rt_ranks, rt_counts)[n][:, :, :]), mid[n][:, 0:NT * NE]
                                 ).then_inc(ranks_kept, 1)
                    exp(b, 3)
                    keep_pt(b, 0)
                    for n in range(1, GT):
                        exp(b, GT + n - 1)
                        keep_pt(b, n)
                    exp(b, BT - 1)
                    weights_hi(B - 1, EB - 1)
                else:
                    keep_pt(b, 0)
                    exp(b, BT - 2)
                    keep_pt(b, 1)
                    keep_pt(b, 2)
                    exp(b, BT - 1)
                    keep_pt(b, 3)
                keep_pt(b, GT)

            def second_half(b, following):
                if following is not None:
                    split_q_hi(following, 0)
                else:
                    load_table(ACT.Silu)
                for n in range(GT + 1, STEPS):
                    keep_pt(b, n)
                    if following is not None and n > GT + 1:
                        exp(following, n - GT - 2)
                        if n == GT + 2:
                            split_q_hi(following, 1)

            phase_c(act, first_half, second_half)

            def step(p, q, loop=False):
                if live(p - 2, loop):
                    act.wait_ge(ey_done, p - 1)
                    act.wait_ge(y_added[q], 16 * (p - 2 - q))
                    n = used(p - 2)
                    act.copy(flat(y[q][:, 0:n, :]), acc[q][:, 0:n * P]).then_inc(y_ready, 1)
                if live(p, loop):
                    n = used(p)
                    act.wait_ge(egu_done, 2 * p + n)
                    act.wait_ge(eh_ready, max(p - 1, 0) if not loop else p - 1)
                    act.activation(esg[q][:, 0:n, :], big[q][:, :].rearrange("p (v f) -> p v f", v=2)[:, 0:n, 0:FE],
                                   ACT.Silu).then_inc(esg_ready, 1)
                if live(p + 2, loop):
                    rowsh_ready(p + 2, q)

            def rowsh_ready(p, q):
                act.wait_ge(xet_done, p + 1)
                n = used(p)
                act.copy(flat(xeh[q][:, 0:n, :]), mid[0][:, 0:n * P]).then_inc(xeh_ready, 1)

            for q in range(2):
                rowsh_ready(q, q)
            phase_d(act, step)

        @block.tensor
        def _(pe):
            def product(dst, weights, moving):
                (wh, wl), (mh, ml) = weights, moving
                pe.matmul(dst, wh, mh, start=True, stop=False)
                pe.matmul(dst, wh, ml, start=False, stop=False)
                return pe.matmul(dst, wl, mh, start=False, stop=True)

            def small(a0, a1):
                return wsh[:, a0 - QK0:a1 - QK0], wsl[:, a0 - QK0:a1 - QK0]

            def warm_up(n):
                for _ in range(n):
                    pe.transpose(mid[0][:, 0:P], identf[:, :], identf[:, :])

            def transpose_x(b, u):
                pe.wait_ge(shared_added[u], FIRST + b)
                for t in range(GT):
                    pe.wait_ge(xn_ready[u], b * GT + t + 1)
                    last = pe.transpose(acc[u][:, t * P:(t + 1) * P], xn[u][:, t, :], identf[:, :])
                last.then_inc(xt_done[u], 1)

            def project_x(b, u):
                pe.wait_ge(xt_kept[u], b + 1)
                pe.wait_ge(vr_kept[1 - u], FIRST + 2 * (b + u))
                for t in range(GT):
                    dst = mid[0][:, t * VR:(t + 1) * VR] if t < GT - 1 else acc[u][:, 0:VR]
                    last = pe.matmul(dst, xt[:, t * P:(t + 1) * P], ws_raw[:, 0:VR], start=True, stop=True)
                last.then_inc(vr_done[u], 1)
                if isinstance(b, int) and b == 0 and u == 0:
                    pe.wait_ge(wsl_ready, 1)
                pe.wait_ge(xtl_ready[u], b + 1)
                pe.wait_ge(qk_kept[1 - u], FIRST + b + u)
                product(mid[1][:, :], small(QK0, QK0 + P), (xth[u][:, :], xtl[u][:, :])).then_inc(qk_done[u], 1)

            def gate_up(b, u, c):
                pe.wait_ge(h_ready[c], FIRST + 2 * b + u)
                for n, w0 in enumerate((GATE0, UP0)):
                    last = product(big[c][:, n * GC:(n + 1) * GC], small(w0 + c * P, w0 + (c + 1) * P),
                                   (xth[u][:, :], xtl[u][:, :]))
                last.then_inc(gu_done[c], 1)

            def down(b, u):
                pe.wait_ge(vr_kept[u], FIRST + 2 * b + 2)
                for c in range(FC):
                    pe.wait_ge(h_ready[c], FIRST + 2 * b + u + 1)
                for t in range(GT):
                    for c in range(FC):
                        cols = slice(t * P, (t + 1) * P)
                        last = pe.matmul(acc[u][:, cols], h[c][:, cols],
                                         ws_raw[:, DOWN0 + c * P:DOWN0 + (c + 1) * P], start=c == 0,
                                         stop=c == FC - 1)
                last.then_inc(ffn_done, 1)

            def step(b, more):
                project_x(b, 0)
                if not (isinstance(b, int) and b == 0):
                    down(b - 1, 1)
                gate_up(b, 0, 0)
                transpose_x(b, 1)
                gate_up(b, 0, 1)
                project_x(b, 1)
                down(b, 0)
                gate_up(b, 1, 0)
                if more:
                    transpose_x(b + 1, 0)
                gate_up(b, 1, 1)

            pe.wait_ge(const_made, 2)
            warm_up(12)
            pe.wait_ge(ws_loaded, 16)
            pe.matmul(mid[1][:, 0:P], ws_raw[0:KD, V10:V10 + P], ws_raw[0:KD, V20:V20 + P], start=True, stop=True
                      ).then_inc(v12_done, 1)
            warm_up(16)
            transpose_x(0, 0)
            pe.wait_ge(v12_kept, 1)
            phase_a(pe, step)
            def rank():
                pe.wait_ge(const_made, CONSTS)
                pe.wait_ge(onehot_ready, B)
                pe.matmul(mid[0][:, 0:NT * NE], before[:, :], flat(onehot[:, :, :]), start=True, stop=True)
                pe.matmul(mid[1][:, 0:NT * NE], onesb[:, :], flat(onehot[:, :, :]), start=True, stop=True
                          ).then_inc(ranked, 1)

            def transpose_rows(p, q):
                pe.wait_ge(xe_loaded[q], 8 * (p - q) + 16)
                pe.wait_ge(xel_ready, p)
                for v in range(used(p)):
                    last = pe.transpose(mid[0][:, v * P:(v + 1) * P], xe[q][:, v, 0:P], identf[:, :])
                last.then_inc(xet_done, 1)

            def scores(b, i):
                if i % GT == 0:
                    pe.wait_ge(q_lo_ready, 2 * b + i // GT + 1)
                    pe.wait_ge(k_lo_ready, FIRST + 2 * b + i // GT + 1)
                if isinstance(b, int) and b == 0 and i < 2:
                    pe.wait_ge(h_ready[i], FIRST + 2 * B)
                pe.wait_ge(exp_done, FIRST + b * BT + max(i - 1, 0))
                q = q_hl[:, i * P:(i + 1) * P]
                for k0 in range(0, (i + 1) * P, GC):
                    k1 = min(k0 + GC, (i + 1) * P)
                    dst = big[i % 2][:, k0:k1]
                    pe.matmul(dst, q, k_hi[:, k0:k1], start=True, stop=False)
                    if k1 == (i + 1) * P:
                        pe.matmul(big[i % 2][:, i * P:k1], identb[:, :], causal[:, :], start=False, stop=False)
                    last = pe.matmul(dst, q, k_lo[:, k0:k1], start=False, stop=True)
                last.then_inc(s_done, 1)

            def transposes(b, n):
                kb, c0 = block_of(n)
                g = 0 if n < GT else 1
                pe.wait_ge(exp_done, FIRST + b * BT + (g + 1) * GT)
                pe.wait_ge(pt_ready, FIRST + b * STEPS + max(n - 1, 0))
                for r in range(c0 // P, GT):
                    last = pe.transpose(mid[n % 2][:, r * P:(r + 1) * P],
                                        prob[g * GT + r][:, kb * P:(kb + 1) * P], identf[:, :])
                last.then_inc(pt_done, 1)

            def weigh(b, n):
                kb, c0 = block_of(n)
                g = 0 if n < GT else 1
                if kb == 0:
                    pe.wait_ge(att_added[g], FIRST + b)
                pe.wait_ge(pt_ready, FIRST + b * STEPS + n + 1)
                v = flat(vr_all[:, bass.ds(b * BT + kb, 1), 0:P])
                for r in range(c0 // P, GT):
                    cols = slice(r * P, (r + 1) * P)
                    last = pe.matmul(acc[g][:, cols], pt[n % 2][:, cols], v, start=kb == 0 and r == 0,
                                     stop=True, skip_group_check=True)
                last.then_inc(pv_done, 1)

            def first_half(b, first):
                if first:
                    for i in range(GT):
                        scores(b, i)
                        if i == 0:
                            rank()
                        if i == 1:
                            down(B - 1, 1)
                    scores(b, GT)
                    pe.wait_ge(ranks_kept, 2)
                    transposes(b, 0)
                else:
                    transposes(b, 0)
                    scores(b, BT - 1)
                for n in range(GT):
                    if first and n + 1 < GT:
                        scores(b, GT + n + 1)
                    if first and n == GT - 1:
                        weigh(b, n)
                        warm_up(12)
                        transposes(b, n + 1)
                    else:
                        transposes(b, n + 1)
                        weigh(b, n)

            def second_half(b, following):
                for n in range(GT, STEPS):
                    if n + 1 < STEPS:
                        transposes(b, n + 1)
                    if following is None and n == STEPS - 2:
                        pe.wait_ge(pt_ready, FIRST + b * STEPS + n + 1)
                        transpose_rows(0, 0)
                    if following is not None and n > GT + 1:
                        scores(following, n - GT - 1)
                    weigh(b, n)
                    if following is not None and n == GT + 1:
                        scores(following, 0)

            phase_c(pe, first_half, second_half)

            words = step_experts[0:1, :].bitcast(I32)
            word = [None]

            def experts(p, q):
                if q == 0:
                    word[0] = pe.value_load(words[0:1, bass.ds(p // 2, 1)])
                e = [pe.snap((word[0] >> (4 * q + n) * CODE) & (NE - 1)) for n in range(4)]
                return e[:2], e[2:]

            def gate_up(p, q, v, e, loop):
                if v == 0:
                    pe.wait_ge(xel_ready, p + 1)
                    pe.wait_ge(eh_ready, p - 1 if loop else max(p - 1, 0))
                w = [flat(m[:, bass.ds(e[v], 1), :]) for m in (weh, wel)]
                product(big[q][:, v * GC:(v + 1) * GC], (xeh[q][:, v, :], xel[q][:, v, :]), w
                        ).then_inc(egu_done, 1)

            def transpose_hidden(p, q):
                pe.wait_ge(eh_ready, p + 1)
                pe.wait_ge(eht_ready, p)
                for v in range(used(p)):
                    for c in range(FC):
                        n = v * FC + c
                        last = pe.transpose(mid[1][:, n * P:(n + 1) * P], eh[q][:, v, c * P:(c + 1) * P],
                                            identf[:, :])
                last.then_inc(eht_done, 1)

            def down(p, q, e):
                pe.wait_ge(eht_ready, p + 1)
                pe.wait_ge(y_ready, p)
                if isinstance(p, int) and p < 2:
                    pe.wait_ge(att_added[q], FIRST + B)
                for v in range(used(p)):
                    for c in range(FC):
                        last = pe.matmul(acc[q][:, v * P:(v + 1) * P], eht[q][:, v, c, :],
                                         flat(wed[:, bass.ds(e[v], 1), c * P:(c + 1) * P]), start=c == 0,
                                         stop=c == FC - 1)
                last.then_inc(ey_done, 1)

            def step(p, q, loop=False):
                e, e_before = experts(p, q)
                if live(p, loop):
                    for v in range(used(p)):
                        gate_up(p, q, v, e, loop)
                if live(p - 2, loop):
                    down(p - 2, q, e_before)
                if live(p - 1, loop):
                    transpose_hidden(p - 1, 1 - q)
                if live(p + 2, loop):
                    transpose_rows(p + 2, q)

            pe.wait_ge(wel_ready, NE)
            pe.wait_ge(wed_loaded, 16)
            pe.wait_ge(experts_ready, 1)
            transpose_rows(1, 1)
            phase_d(pe, step)


CONSTS = 11
ROUND = float(1 << 23)
CODE = 4
AHEAD = 4
FIRST = 1


def block_of(n):
    kb = n if n < GT else n - GT
    return kb, (kb if n < GT else max(kb - GT, 0)) * P


def kernel(L0_attn_x, L0_attn_w_q, L0_attn_w_k, L0_attn_w_v1, L0_attn_w_v2, L0_ffn_w_router,
           L0_ffn_gate_up_proj, L0_ffn_down_proj, L0_ffn_w_gate, L0_ffn_w_up, L0_ffn_w_down):
    import concourse.bacc as bacc
    from concourse.bass_utils import run_bass_kernel_spmd

    x = np.ascontiguousarray(L0_attn_x)
    F = L0_ffn_w_down.shape[1]
    E = L0_ffn_down_proj.shape[0]
    w_down = np.transpose(L0_ffn_w_down).reshape(F // P, P, P).transpose(1, 0, 2).reshape(P, F)
    w_v1t, w_v2 = (np.concatenate([w, w], axis=0) for w in (np.transpose(L0_attn_w_v1), L0_attn_w_v2))
    w_small = np.ascontiguousarray(np.concatenate([
        w_v1t, np.transpose(L0_ffn_w_router), L0_attn_w_q, L0_attn_w_k, np.transpose(L0_ffn_w_gate),
        np.transpose(L0_ffn_w_up), w_down, w_v2], axis=1))
    gate_up = np.transpose(L0_ffn_gate_up_proj, (1, 0, 2))
    down = np.reshape(L0_ffn_down_proj, (E, F // P, P, P)).transpose(2, 0, 1, 3).reshape(P, E, F)

    n_tokens = x.shape[0] * x.shape[1]
    slot_tiles = n_tokens // P + E
    nc = bacc.Bacc("TRN2", target_bir_lowering=False, num_devices=1)
    arrays = {"x": x, "w_small": w_small, "w_gate_up": np.ascontiguousarray(gate_up),
              "w_down": np.ascontiguousarray(down)}
    args = [nc.dram_tensor(n, a.shape, F32, kind="ExternalInput").ap() for n, a in arrays.items()]
    scratch = nc.dram_tensor("scratch", (slot_tiles * P, P + 1), F32, kind="Internal").ap()
    out = nc.dram_tensor("out", x.shape, F32, kind="ExternalOutput").ap()
    build(nc, *args, scratch, out)
    return run_bass_kernel_spmd(nc, [arrays], core_ids=[0]).results[0]["out"]
```
